# Optimizing a Trainium2 kernel written in Bass

```python
import numpy as np
import jax
import jax.numpy as jnp

def _softmax(x, axis=-1):
    return jax.nn.softmax(x, axis=axis)

def _gelu(x):
    return jax.nn.gelu(x, approximate=True)

def _silu(x):
    return jax.nn.silu(x)

def _sigmoid(x):
    return jax.nn.sigmoid(x)

def _layernorm(x, axis=-1, eps=1e-05):
    m = jnp.mean(x, axis=axis, keepdims=True)
    v = jnp.var(x, axis=axis, keepdims=True)
    return (x - m) / jnp.sqrt(v + eps)

def _scatter_add(tgt, idx, src, axis=0):
    return tgt.at[idx].add(src)

def _segment_sum(src, seg, n):
    return jax.ops.segment_sum(src, seg, n)
kernel_name = 'mk_macaron_d1_jaxref_r8_86c20f'

def setup_inputs(seed: int=0):
    np.random.seed(seed)
    _w = jnp.asarray

    def _L0_attn_setup():
        import jax, jax.numpy as jnp
        import numpy as np
        H = 512
        D = H // 4
        key = jax.random.key(seed)
        k1, k2, k3, k4, k5 = jax.random.split(key, 5)
        x = jax.random.normal(k1, (4, 512, H), dtype=jnp.float32)
        s_in = 1.0 / np.sqrt(H)
        Wqkv = jax.random.normal(k2, (H, 3 * D), dtype=jnp.float32) * s_in
        bqkv = jax.random.normal(k3, (3 * D,), dtype=jnp.float32) * 0.01
        Wo = jax.random.normal(k4, (D, H), dtype=jnp.float32) * (1.0 / np.sqrt(D))
        bo = jax.random.normal(k5, (H,), dtype=jnp.float32) * 0.01
        return {'x': x, 'Wqkv': Wqkv, 'bqkv': bqkv, 'Wo': Wo, 'bo': bo}
    _L0_attn_in = _L0_attn_setup()

    def _L0_ffn_setup():
        import jax, jax.numpy as jnp
        import numpy as np
        DIM = 512
        INTER = 128
        E = 16
        GROUPS = 4
        LIM = 2
        K = 2
        SHARED_INTER = 2 * INTER
        SCALE = 1.0
        key = jax.random.key(seed)
        ks = jax.random.split(key, 16)

        def n(k, shape, s=0.02):
            return jax.random.normal(k, shape, jnp.float32) * s
        return {'x': jax.random.normal(ks[0], (1, 256, DIM), jnp.float32), 'router_w': n(ks[1], (DIM, E)), 'router_b': n(ks[2], (E,)), 'router_bias': n(ks[3], (E,), 1.0), 'ew1': n(ks[4], (E, DIM, INTER)), 'eb1': n(ks[5], (E, INTER)), 'ew2': n(ks[6], (E, DIM, INTER)), 'eb2': n(ks[7], (E, INTER)), 'ew3': n(ks[8], (E, INTER, DIM)), 'eb3': n(ks[9], (E, DIM)), 'sw1': n(ks[10], (DIM, SHARED_INTER)), 'sb1': n(ks[11], (SHARED_INTER,)), 'sw2': n(ks[12], (DIM, SHARED_INTER)), 'sb2': n(ks[13], (SHARED_INTER,)), 'sw3': n(ks[14], (SHARED_INTER, DIM)), 'sb3': n(ks[15], (DIM,))}
    _L0_ffn_in = _L0_ffn_setup()
    _d = {'L0_attn_x': _L0_attn_in['x'], 'L0_attn_Wqkv': _L0_attn_in['Wqkv'], 'L0_attn_bqkv': _L0_attn_in['bqkv'], 'L0_attn_Wo': _L0_attn_in['Wo'], 'L0_attn_bo': _L0_attn_in['bo'], 'L0_ffn_router_w': _L0_ffn_in['router_w'], 'L0_ffn_router_b': _L0_ffn_in['router_b'], 'L0_ffn_router_bias': _L0_ffn_in['router_bias'], 'L0_ffn_ew1': _L0_ffn_in['ew1'], 'L0_ffn_eb1': _L0_ffn_in['eb1'], 'L0_ffn_ew2': _L0_ffn_in['ew2'], 'L0_ffn_eb2': _L0_ffn_in['eb2'], 'L0_ffn_ew3': _L0_ffn_in['ew3'], 'L0_ffn_eb3': _L0_ffn_in['eb3'], 'L0_ffn_sw1': _L0_ffn_in['sw1'], 'L0_ffn_sb1': _L0_ffn_in['sb1'], 'L0_ffn_sw2': _L0_ffn_in['sw2'], 'L0_ffn_sb2': _L0_ffn_in['sb2'], 'L0_ffn_sw3': _L0_ffn_in['sw3'], 'L0_ffn_sb3': _L0_ffn_in['sb3']}
    _x0 = _d['L0_attn_x']
    _d['L0_attn_x'] = jax.random.normal(jax.random.fold_in(jax.random.key(seed), 1), (4, 512, 512), dtype=_x0.dtype)
    del _x0
    return _d

def reference(L0_attn_x, L0_attn_Wqkv, L0_attn_bqkv, L0_attn_Wo, L0_attn_bo, L0_ffn_router_w, L0_ffn_router_b, L0_ffn_router_bias, L0_ffn_ew1, L0_ffn_eb1, L0_ffn_ew2, L0_ffn_eb2, L0_ffn_ew3, L0_ffn_eb3, L0_ffn_sw1, L0_ffn_sb1, L0_ffn_sw2, L0_ffn_sb2, L0_ffn_sw3, L0_ffn_sb3):

    def _L0_attn_ref(x, Wqkv, bqkv, Wo, bo):
        import jax, jax.numpy as jnp
        import numpy as np
        H = 512
        D = H // 4
        B, S, C = x.shape
        d = C // 4
        qkv = jnp.einsum('bsc,cf->bsf', x, Wqkv) + bqkv
        qkv = qkv.reshape(B, S, 3, d)
        q, k, v = (qkv[:, :, 0], qkv[:, :, 1], qkv[:, :, 2])
        scale = 1.0 / jnp.sqrt(jnp.float32(d)).astype(x.dtype)
        attn = jnp.einsum('bqd,bkd->bqk', q, k) * scale
        attn = jax.nn.softmax(attn, axis=-1)
        out = jnp.einsum('bqk,bkd->bqd', attn, v)
        return jnp.einsum('bqd,dc->bqc', out, Wo) + bo

    def _L0_ffn_ref(x, router_w, router_b, router_bias, ew1, eb1, ew2, eb2, ew3, eb3, sw1, sb1, sw2, sb2, sw3, sb3):
        import jax, jax.numpy as jnp
        import numpy as np
        DIM = 512
        INTER = 128
        E = 16
        GROUPS = 4
        LIM = 2
        K = 2
        SHARED_INTER = 2 * INTER
        SCALE = 1.0
        shape = x.shape
        xt = x.reshape(-1, DIM)
        T = xt.shape[0]
        logits = xt @ router_w + router_b
        scores = jax.nn.softmax(logits.astype(jnp.float32), axis=-1) + router_bias
        g = scores.reshape(T, GROUPS, E // GROUPS)
        _, gidx = jax.lax.top_k(g.max(axis=-1), LIM)
        keep = jnp.zeros((T, GROUPS), bool).at[jnp.arange(T)[:, None], gidx].set(True)
        masked = jnp.where(keep[:, :, None], g, -jnp.inf).reshape(T, E)
        _, idx = jax.lax.top_k(masked, K)
        vals = (jnp.take_along_axis(scores, idx, axis=1) * SCALE).astype(x.dtype)
        gate = jnp.zeros((T, E), x.dtype).at[jnp.arange(T)[:, None], idx].add(vals)

        def step(y, p):
            w1, b1, w2, b2, w3, b3, ge = p
            h = jax.nn.silu(xt @ w1 + b1) * (xt @ w2 + b2)
            return (y + ge[:, None] * (h @ w3 + b3), None)
        y, _ = jax.lax.scan(step, jnp.zeros_like(xt), (ew1, eb1, ew2, eb2, ew3, eb3, gate.T))
        z = jax.nn.silu(xt @ sw1 + sb1) * (xt @ sw2 + sb2) @ sw3 + sb3
        return (y + z).reshape(shape)
    x = L0_attn_x
    x = x + 0.5 * _L0_ffn_ref(_layernorm(x, axis=-1), L0_ffn_router_w, L0_ffn_router_b, L0_ffn_router_bias, L0_ffn_ew1, L0_ffn_eb1, L0_ffn_ew2, L0_ffn_eb2, L0_ffn_ew3, L0_ffn_eb3, L0_ffn_sw1, L0_ffn_sb1, L0_ffn_sw2, L0_ffn_sb2, L0_ffn_sw3, L0_ffn_sb3)
    x = x + _L0_attn_ref(_layernorm(x, axis=-1), L0_attn_Wqkv, L0_attn_bqkv, L0_attn_Wo, L0_attn_bo)
    x = x + 0.5 * _L0_ffn_ref(_layernorm(x, axis=-1), L0_ffn_router_w, L0_ffn_router_b, L0_ffn_router_bias, L0_ffn_ew1, L0_ffn_eb1, L0_ffn_ew2, L0_ffn_eb2, L0_ffn_ew3, L0_ffn_eb3, L0_ffn_sw1, L0_ffn_sb1, L0_ffn_sw2, L0_ffn_sb2, L0_ffn_sw3, L0_ffn_sb3)
    return x

_drawn_inputs = setup_inputs


def setup_inputs(seed=0):
    import zlib

    import numpy as np

    out = dict(_drawn_inputs(seed))
    spreads = {}
    factors = {'L0_attn_bqkv': 5.206,
     'L0_attn_bo': 5.815,
     'L0_ffn_router_w': 8.0,
     'L0_ffn_router_b': 198.504,
     'L0_ffn_eb1': 8.0,
     'L0_ffn_eb2': 8.0,
     'L0_ffn_sb1': 33.4,
     'L0_ffn_sb2': 32.104}
    for name, (base, spread) in spreads.items():
        noise = np.random.default_rng([zlib.crc32(name.encode()), seed]).standard_normal(out[name].shape)
        drawn = base * np.exp(spread * noise) if base else spread * noise
        out[name] = jnp.asarray(drawn.astype(out[name].dtype))
    for name, factor in factors.items():
        out[name] = (out[name] * factor).astype(out[name].dtype)
    return out
```

```python
import concourse.bass as bass
from concourse import mybir
from contextlib import ExitStack

P = 128
D = 512
KC = D // P
T = 2048
NT = T // P
G = 4
GT = NT // G
GW = GT * P
E = 16
EG = 4
TOPK = 2
FI = 128
SI = 256
SF = SI // P
HD = 128
EPS = 1e-5
SCALE = float(HD) ** -0.5
NB = (TOPK * T + E * (P - 1)) // P
NBP = NB + 1
RING = 4
LOW = -3.0e38
OUTSIDE = 1 << 20

C_ID, C_R, C_B = 0, 128, 256
C_REV16 = C_B + NBP
C_REV4 = C_REV16 + 16
C_THR = C_REV4 + 4
C_TK = C_THR + 16
C_P = C_TK + 32
C_EMOD = C_P + 1
C_MASK = C_EMOD + 1
C_SB1 = C_MASK + 3
C_SB2 = C_SB1 + 2
C_BQKV = C_SB2 + 2
C_RB = C_BQKV + 3
C_RBIAS = C_RB + 16
NKEEP = C_RBIAS + 16
S_TRI, S_SELS, S_SELO, S_SELV, S_B12, S_B3 = 0, 128, 256, 384, 512, 768
NONCE = 768 + 512


def macaron_kernel(nc, x_in, keep_in, once_in, rw_in, w12_in, w3_in, sw12_in, sw3_in, wqkv_in, wo_in, out):
    F32, BF16, I32, U32 = mybir.dt.float32, mybir.dt.bfloat16, mybir.dt.int32, mybir.dt.uint32
    ALU, ACT, AX = mybir.AluOpType, mybir.ActivationFunctionType, mybir.AxisListType

    with ExitStack() as ctx:
        def sb(name, shape, dt=F32):
            return ctx.enter_context(nc.sbuf_tensor(name, shape, dt))

        def sem(name):
            return ctx.enter_context(nc.semaphore(name))

        bank = [ctx.enter_context(nc.psum_tensor(f"bank{i}", [P, 512], F32)) for i in range(8)]

        w12 = sb("w12", [P, KC, E * 2 * FI])
        w3 = sb("w3", [P, E * D])
        sw12 = sb("sw12", [P, KC, 2 * SI])
        sw3 = sb("sw3", [P, SF, D])
        rw = sb("rw", [P, KC, E])
        keep = sb("keep", [P, NKEEP])
        x = sb("x", [P, NT, D])
        b12 = sb("b12", [P, 2 * FI], BF16)
        b3 = sb("b3", [P, D], BF16)
        tri = sb("tri", [P, P], BF16)
        ones = sb("ones", [P, P], BF16)
        sel_sb3 = sb("sel_sb3", [P, P], BF16)
        sel_bo = sb("sel_bo", [P, P], BF16)
        sel_bv = sb("sel_bv", [P, P], BF16)
        eoh = sb("eoh", [P, NBP], BF16)
        gates = sb("gates", [P, TOPK, NT])
        eid = sb("eid", [1, NBP], I32)
        gidx = sb("gidx", [P, NBP], U32)
        sidx = sb("sidx", [P, NBP], U32)
        gi = sb("gi", [P, RING], U32)
        si = sb("si", [P, RING], U32)
        st6 = sb("st6", [P, GT, 6])
        mv = sb("mv", [P, GT, 2])
        veps = sb("veps", [P, GT])
        rstd = sb("rstd", [P, GT])
        mhalf = sb("mhalf", [P, GT])
        slot_f = sb("slot_f", [P, TOPK * NT])
        slot_i = sb("slot_i", [P, TOPK * NT], I32)
        r_i = sb("r_i", [P, TOPK * NT], I32)
        b_i = sb("b_i", [P, TOPK * NT], I32)
        r_f = sb("r_f", [P, TOPK * NT])
        b_f = sb("b_f", [P, TOPK * NT])
        nmax = sb("nmax", [P, GT])
        rsum = sb("rsum", [P, GT])
        rinv = sb("rinv", [P, GT])
        s16 = sb("s16", [P, 16 * 6])
        xn = sb("xn", [P, 2, D])
        xT = sb("xT", [P, 3, KC, GW])
        shared = sb("shared", [P, 4 * 512])
        work = sb("work", [P, 5888])

        sh_h = shared[:, 0:1024].rearrange("p (f n) -> p f n", f=SF)
        sh_u = shared[:, 1024:1536]
        yin = shared[:, :].rearrange("p (s k n) -> p s k n", s=2, k=2)
        wqkv = work[:, 0:1536].rearrange("p (c n) -> p c n", c=KC)
        wo = work[:, 1536:2048]
        qT, kT = work[:, 2048:2560], work[:, 2560:3072]
        v = work[:, 3072:3584].rearrange("p (t n) -> p t n", t=GT)
        prob = work[:, 3584:4608].rearrange("p (s n) -> p s n", s=2)
        pT = work[:, 4608:5632].rearrange("p (s t n) -> p s t n", s=2, t=GT)
        oT = work[:, 5632:5888].rearrange("p (s n) -> p s n", s=2)
        sh_z = work[:, 4608:5632].rearrange("p (s n) -> p s n", s=2)
        ex1 = xT[:, 1, :, :].rearrange("p c n -> p (c n)")
        ex2 = xT[:, 2, :, :].rearrange("p c n -> p (c n)")
        xg = work[:, 2048:4096].rearrange("p (s n) -> p s n", s=RING)
        xgT = ex1[:, 0:1024].rearrange("p (s c n) -> p s c n", s=2, c=KC)
        yo = ex2[:, :].rearrange("p (s n) -> p s n", s=RING)
        e_silu = ex1[:, 1024:1280].rearrange("p (s n) -> p s n", s=2)
        e_h = ex1[:, 1280:1536].rearrange("p (s n) -> p s n", s=2)
        e_hT = ex1[:, 1536:1792].rearrange("p (s n) -> p s n", s=2)

        ident = keep[:, C_ID:C_ID + P]

        xn_d = [nc.dram_tensor(f"xn_d{l}", [T, D], F32) for l in range(2)]
        y_d = [nc.dram_tensor(f"y_d{l}", [TOPK * T, D], F32) for l in range(2)]

        keep_in_s, once_s, rw_s, x_s = sem("keep_loaded"), sem("once_loaded"), sem("rw_loaded"), [sem(f"x_loaded{g}") for g in range(G)]
        sw12_s, sw3_s, w12_s, w3_s = sem("sw12_loaded"), sem("sw3_loaded"), sem("w12_loaded"), sem("w3_loaded")
        attw_s = sem("attn_weights_loaded")
        consts_s = sem("consts_ready")
        mhalf_s = sem("mhalf_ready")
        vstep = sem("vector_step")
        var_s = sem("variance_ready")
        rstd_s = sem("rstd_ready")
        xn_s = sem("xn_ready")
        xn_out = [sem("xn_stored0"), sem("xn_stored1")]
        tr_s = sem("transposed")
        trc_s = sem("transposed_copied")
        logit_s = sem("logits_done")
        gu_s = sem("shared_gate_up_done")
        shact_s = sem("shared_act_done")
        shmul_s = sem("shared_mul_done")
        z_s = sem("shared_out_done")
        zc_s = sem("shared_out_copied")
        zadd_s = sem("shared_added")
        lb_s = sem("router_exp_in")
        ex_s = sem("router_exp_done")
        chosen_s = sem("chosen_ready")
        prefix_s = sem("prefix_done")
        onehot_s = sem("onehots_ready")
        table_s = sem("table_done")
        index_s = sem("indices_ready")
        gi_s, si_s = sem("gather_index"), sem("scatter_index")
        started_s = sem("indirect_dmas_started")
        got_s = [sem(f"gathered{s}") for s in range(RING)]
        put_s = [sem(f"scattered{s}") for s in range(RING)]
        gT_s, gTc_s = sem("block_transposed"), sem("block_transposed_copied")
        egu_s, esilu_s, eh_s = sem("block_gate_up"), sem("block_silu"), sem("block_h")
        ehT_s, ehTc_s = sem("block_h_transposed"), sem("block_h_transposed_copied")
        ed_s, yo_s = sem("block_down"), sem("block_out_ready")
        yin_s = [sem("results_loaded0"), sem("results_loaded1")]
        comb_s = sem("combined")
        qkv_s, qkvc_s = sem("qkv_done"), sem("qkv_copied")
        sc_s, nmax_s, exp_s, prob_s = sem("scores_done"), sem("row_max_ready"), sem("exp_done"), sem("probs_ready")
        pv_s, pvc_s, o_s, att_s = sem("pv_done"), sem("pv_copied"), sem("attn_out_done"), sem("attn_added")
        out_s = sem("out_stored")

        LN_ORDER = [("f0", 0), ("f0", 1), ("f0", 2), ("f0", 3), ("a", 0), ("a", 1), ("f1", 0), ("a", 2), ("f1", 1),
                    ("a", 3), ("f1", 2), ("f1", 3)]
        LN_AT = {key: GT * n for n, key in enumerate(LN_ORDER)}
        TR_ORDER = [("f0", 0), ("f0", 1), ("f0", 2), ("f0", 3), ("a", 0), ("a", 1), ("p", 0), ("f1", 0), ("a", 2), ("p", 1),
                    ("f1", 1), ("a", 3), ("p", 2), ("f1", 2), ("p", 3), ("f1", 3)]
        TR_AT = {key: GT * n for n, key in enumerate(TR_ORDER)}
        def stores_before(kind, g, i):
            n = 0
            for key in LN_ORDER:
                for j in range(GT):
                    if key == (kind, g) and j == i:
                        return n
                    if key[0] != "a" and j % 2 == i % 2:
                        n += 1
        XT_SLOT = {("f0", g): g % 3 for g in range(G)} | {("a", g): 2 for g in range(G)} | {("f1", g): g % 3 for g in range(G)}
        SH = lambda l, g: l * G + g
        ring_base = lambda l, s: 16 * l * ((NB - s + RING - 1) // RING)
        ring_count = lambda l, b, s: b * (16 // RING) + (ring_base(l, s) - s * (16 // RING))

        block = ctx.enter_context(nc.Block())

        @block.sync
        def _(sp):
            def load_results(l, g):
                yv = y_d[l].rearrange("(k t p) n -> t p k n", k=TOPK, p=P)
                for i in range(GT):
                    n = l * NT + g * GT + i
                    if n % NT == 0:
                        for s in range(RING):
                            sp.wait_ge(put_s[s], ring_base(l + 1, s))
                        sp.wait_ge(z_s, GT * G * (l + 1))
                        sp.wait_ge(shmul_s, SF * G * (l + 1))
                    if n % NT >= 2:
                        sp.wait_ge(comb_s, n - 1)
                    sp.dma_start(yin[:, i % 2, :, :], yv[g * GT + i]).then_inc(yin_s[i % 2], 16)

            def store_out(g):
                for t in range(g * GT, (g + 1) * GT):
                    sp.wait_ge(comb_s, NT + t + 1)
                    sp.dma_start(out[t * P:(t + 1) * P, :], x[:, t, :]).then_inc(out_s, 16)

            xv = x_in.rearrange("(t p) n -> p t n", p=P)
            sp.dma_start(x[:, 0:GT, :], xv[:, 0:GT, :]).then_inc(x_s[0], 16)
            sp.dma_start(keep[:, :], keep_in).then_inc(keep_in_s, 16)
            sp.dma_start(rw[:, :, :], rw_in).then_inc(rw_s, 16)
            sp.dma_start(sw12[:, :, :], sw12_in).then_inc(sw12_s, 16)
            sp.dma_start(x[:, GT:2 * GT, :], xv[:, GT:2 * GT, :]).then_inc(x_s[1], 16)
            sp.dma_start(work[:, 0:NONCE], once_in).then_inc(once_s, 16)
            sp.dma_start(sw3[:, :, :], sw3_in).then_inc(sw3_s, 16)
            for g in range(2, G):
                sp.dma_start(x[:, g * GT:(g + 1) * GT, :], xv[:, g * GT:(g + 1) * GT, :]).then_inc(x_s[g], 16)
            sp.wait_ge(index_s, 1)
            sp.dma_start(wqkv, wqkv_in).then_inc(attw_s, 16)
            sp.dma_start(wo, wo_in).then_inc(attw_s, 16)
            load_results(0, 0)
            load_results(0, 1)
            load_results(0, 2)
            load_results(0, 3)
            for g in range(G):
                load_results(1, g)
                if g:
                    store_out(g - 1)
            store_out(G - 1)
            sp.wait_ge(out_s, 16 * NT)

        @block.gpsimd
        def _(pool):
            def rsqrt(n):
                pool.wait_ge(var_s, n + 1)
                pool.tensor_tensor(rstd[:, :], veps[:, :], mhalf[:, :], ALU.pow).then_inc(rstd_s, 1)

            def shared_part(l, g):
                u = SH(l, g)
                for f in range(SF):
                    pool.wait_ge(shact_s, u * 2 * SF + 2 * f + 2)
                    pool.tensor_tensor(sh_h[:, f, :], sh_h[:, f, :], sh_u, ALU.mult).then_inc(shmul_s, 1)
                for i in range(GT):
                    t = g * GT + i
                    pool.wait_ge(zc_s, u * GT + i + 1)
                    pool.tensor_tensor(x[:, t, :], x[:, t, :], sh_z[:, i % 2, :], ALU.add).then_inc(zadd_s, 1)

            last_token, last_result = pool.to_reg(T - 1), pool.to_reg(TOPK * T - 1)

            def gather(l, b, s):
                pool.tensor_copy(gi[:, s:s + 1], gidx[:, bass.ds(b, 1)]).then_inc(gi_s, 1)
                pool.wait_ge(gi_s, b + (l * NB + 1))
                pool.sem_inc(started_s)
                pool.indirect_dma_start(xg[:, s, :], None, xn_d[l][:, :], bass.IndirectOffsetOnAxis(ap=gi[:, s:s + 1], axis=0),
                                        bounds_check=last_token, oob_is_err=False).then_inc(got_s[s], 16)

            def scatter(l, b, s):
                pool.wait_ge(yo_s, l * NB + b + 1)
                pool.tensor_copy(si[:, s:s + 1], sidx[:, bass.ds(b, 1)]).then_inc(si_s, 1)
                pool.wait_ge(si_s, b + (l * NB + 1))
                pool.sem_inc(started_s)
                pool.indirect_dma_start(y_d[l][:, :], bass.IndirectOffsetOnAxis(ap=si[:, s:s + 1], axis=0), yo[:, s, :], None,
                                        bounds_check=last_result, oob_is_err=False).then_inc(put_s[s], 16)

            def experts(l):
                pool.wait_ge(index_s, l + 1)
                for s in range(2):
                    pool.wait_ge(xn_out[s], 16 * (l + 1) * NT // 2)
                for s in range(RING):
                    gather(l, s, s)
                whole = (NB - RING) // RING * RING
                with pool.Fori(0, whole, RING) as b:
                    for s in range(RING):
                        pool.wait_ge(gT_s, b + (l * NB + s + 1))
                        gather(l, b + (s + RING), s)
                        scatter(l, b + s, s)
                for b in range(whole, NB):
                    if b + RING < NB:
                        pool.wait_ge(gT_s, l * NB + b + 1)
                        gather(l, b + RING, b % RING)
                    scatter(l, b, b % RING)

            pool.memset(mhalf[:, :], -0.5).then_inc(mhalf_s, 1)
            pool.wait_ge(mhalf_s, 1)
            rsqrt(0)
            rsqrt(1)
            shared_part(0, 0)
            rsqrt(2)
            rsqrt(3)
            for g in range(1, G):
                shared_part(0, g)
            experts(0)
            for n in range(G, len(LN_ORDER)):
                rsqrt(n)
            for g in range(G):
                shared_part(1, g)
            experts(1)

        @block.scalar
        def _(act):
            def copy_T(kind, g, i):
                key = (kind, g)
                k = TR_AT[key] + i
                act.wait_ge(tr_s, k + 1)
                if kind == "p":
                    dst = pT[:, i % 2, :, :]
                else:
                    dst = xT[:, XT_SLOT[key], :, i * P:(i + 1) * P]
                if kind in ("f0", "f1"):
                    t = g * GT + i
                    act.dma_start(xn_d[int(kind[1])][t * P:(t + 1) * P, :], xn[:, i % 2, :]).then_inc(xn_out[i % 2], 16)
                nc.scalar.activation(dst, bank[k % 2][:, :].rearrange("p (c n) -> p c n", c=KC), ACT.Copy).then_inc(trc_s, 1)

            def shared_part(l, g):
                u = SH(l, g)
                for f in range(SF):
                    act.wait_ge(gu_s, u * 2 * SF + 2 * f + 1)
                    if u:
                        act.wait_ge(z_s, u * GT)
                    nc.scalar.activation(sh_h[:, f, :], bank[3][:, :], ACT.Silu, bias=keep[:, C_SB1 + f:C_SB1 + f + 1]).then_inc(shact_s, 1)
                    act.wait_ge(gu_s, u * 2 * SF + 2 * f + 2)
                    if u or f:
                        act.wait_ge(shmul_s, u * SF + f)
                    nc.scalar.activation(sh_u, bank[4][:, :], ACT.Identity, bias=keep[:, C_SB2 + f:C_SB2 + f + 1]).then_inc(shact_s, 1)
                for i in range(GT):
                    n = u * GT + i
                    act.wait_ge(z_s, n + 1)
                    if n >= 2:
                        act.wait_ge(zadd_s, n - 1)
                    nc.scalar.activation(sh_z[:, i % 2, :], bank[6 + i % 2][:, :], ACT.Copy, scale=0.5).then_inc(zc_s, 1)

            def attn_copies(g, n):
                act.wait_ge(qkv_s, 3 * g + n + 1)
                if n < 2:
                    nc.scalar.activation([qT, kT][n], bank[3 + n][:, :], ACT.Identity, bias=keep[:, C_BQKV + n:C_BQKV + n + 1]).then_inc(qkvc_s, 1)
                else:
                    nc.scalar.activation(v, bank[5][:, :].rearrange("p (t n) -> p t n", t=GT), ACT.Copy).then_inc(qkvc_s, 1)

            def exp(g, i):
                act.wait_ge(nmax_s, g * GT + i + 1)
                nc.scalar.activation(prob[:, i % 2, :], bank[3 + i % 2][:, :], ACT.Exp, bias=nmax[:, i:i + 1], scale=SCALE,
                                     accum_out=rsum[:, i:i + 1]).then_inc(exp_s, 1)

            def copy_pv(g, i):
                n = g * GT + i
                act.wait_ge(pv_s, n + 1)
                nc.scalar.activation(oT[:, i % 2, :], bank[6][:, 0:P], ACT.Copy).then_inc(pvc_s, 1)

            def softmax_part(g):
                exp(g, 0)
                exp(g, 1)
                copy_T("p", g, 0)
                for i in range(GT):
                    if i + 2 < GT:
                        exp(g, i + 2)
                    if i + 1 < GT:
                        copy_T("p", g, i + 1)
                    copy_pv(g, i)

            def router_exp(l):
                act.wait_ge(lb_s, l + 1)
                nc.scalar.activation(work[:, 0:NT * E], work[:, 0:NT * E], ACT.Exp).then_inc(ex_s, 1)

            def block_act(l, b, s):
                q = l * NB + b
                act.wait_ge(egu_s, q + 1)
                nc.scalar.activation(e_silu[:, s, :], bank[3 + s][:, 0:FI], ACT.Silu).then_inc(esilu_s, 1)

            def block_copy_T(l, b, s):
                act.wait_ge(gT_s, b + (l * NB + 1))
                nc.scalar.activation(xgT[:, s, :, :], bank[s][:, :].rearrange("p (c n) -> p c n", c=KC), ACT.Copy).then_inc(gTc_s, 1)

            def experts(l):
                block_copy_T(l, 0, 0)
                with act.Fori(0, NB - 1, 2) as b:
                    for s in range(2):
                        block_act(l, b + s, s)
                        block_copy_T(l, b + (s + 1), 1 - s)
                block_act(l, NB - 1, 0)

            act.wait_ge(keep_in_s, 16)
            for i in range(GT):
                copy_T("f0", 0, i)
            act.dma_start(w12[:, :, :], w12_in).then_inc(w12_s, 16)
            act.dma_start(w3[:, :], w3_in).then_inc(w3_s, 16)
            act.wait_ge(consts_s, 1)
            shared_part(0, 0)
            for g in range(1, G):
                for i in range(GT):
                    copy_T("f0", g, i)
            router_exp(0)
            for g in range(1, G):
                shared_part(0, g)
            experts(0)
            for i in range(GT):
                copy_T("a", 0, i)
            attn_copies(0, 0)
            attn_copies(0, 1)
            attn_copies(0, 2)
            for i in range(GT):
                copy_T("a", 1, i)
            softmax_part(0)
            for g in range(1, G):
                last = g == G - 1
                attn_copies(g, 0)
                if not last:
                    copy_T("f1", g - 1, 0)
                    copy_T("f1", g - 1, 1)
                attn_copies(g, 1)
                if not last:
                    copy_T("f1", g - 1, 2)
                    copy_T("f1", g - 1, 3)
                attn_copies(g, 2)
                for i in range(GT):
                    copy_T(*(("f1", g - 1) if last else ("a", g + 1)), i)
                softmax_part(g)
            shared_part(1, 0)
            for i in range(GT):
                copy_T("f1", 3, i)
            router_exp(1)
            for g in range(1, G):
                shared_part(1, g)
            experts(1)

        @block.tensor
        def _(pe):
            def fill_T(kind, g, i):
                k = TR_AT[kind, g] + i
                pe.wait_ge(xn_s, LN_AT[kind, g] + i + 1)
                if k >= 2:
                    pe.wait_ge(trc_s, k - 1)
                for c in range(KC):
                    ins = pe.transpose(bank[k % 2][:, c * P:(c + 1) * P], xn[:, i % 2, c * P:(c + 1) * P], ident)
                ins.then_inc(tr_s, 1)

            def router(l, g, i):
                key = (f"f{l}", g)
                t = g * GT + i
                pe.wait_ge(trc_s, TR_AT[key] + i + 1)
                for c in range(KC):
                    ins = pe.matmul(bank[2][:, t * E:(t + 1) * E], xT[:, XT_SLOT[key], c, i * P:(i + 1) * P], rw[:, c, :],
                                    start=(c == 0), stop=(c == KC - 1))
                if i == GT - 1:
                    ins.then_inc(logit_s, 1)

            def ffn_tiles(l, g, tiles, flush=False):
                for i in tiles:
                    fill_T(f"f{l}", g, i)
                    if i:
                        router(l, g, i - 1)
                if flush:
                    router(l, g, GT - 1)

            def shared_part(l, g):
                u = SH(l, g)
                src = xT[:, XT_SLOT[f"f{l}", g], :, :]
                for m in range(2 * SF):
                    if u * 2 * SF + m >= 2:
                        pe.wait_ge(shact_s, u * 2 * SF + m - 1)
                    col = (m // 2) * P + (m % 2) * SI
                    for c in range(KC):
                        ins = pe.matmul(bank[3 + m % 2][:, :], sw12[:, c, col:col + P], src[:, c, :], start=(c == 0), stop=(c == KC - 1))
                    ins.then_inc(gu_s, 1)
                pe.wait_ge(shmul_s, (u + 1) * SF)
                for i in range(GT):
                    n = u * GT + i
                    if n >= 2:
                        pe.wait_ge(zc_s, n - 1)
                    if l and g == 0 and i == 1:
                        pe.wait_ge(att_s, NT)
                    o = bank[6 + i % 2][:, :]
                    pe.matmul(o, sel_sb3[:, :], b3[:, :], start=True, stop=False)
                    for f in range(SF):
                        ins = pe.matmul(o, sh_h[:, f, i * P:(i + 1) * P], sw3[:, f, :], start=False, stop=(f == SF - 1))
                    ins.then_inc(z_s, 1)

            def prefix(l):
                chosen = work[:, 4480:4608].bitcast(BF16)
                pe.wait_ge(chosen_s, l + 1)
                pe.matmul(bank[0][:, 0:NT * E], tri[:, :], chosen, start=True, stop=True)
                pe.matmul(bank[1][:, 0:NT * E], ones[:, :], chosen, start=True, stop=True).then_inc(prefix_s, 1)

            def table(l):
                ohr = work[:, 0:2048].bitcast(BF16)
                obv = work[:, 2048:2048 + 48 * 32].bitcast(BF16)
                pe.wait_ge(onehot_s, l + 1)
                for n in range(TOPK * NT):
                    ins = pe.matmul(bank[0][:, 0:2 * NBP], ohr[:, n * P:(n + 1) * P], obv[:, n * 2 * NBP:(n + 1) * 2 * NBP],
                                    start=(n == 0), stop=(n == TOPK * NT - 1))
                ins.then_inc(table_s, 1)

            def qkv(g, n):
                src = xT[:, XT_SLOT["a", g], :, :]
                if n == 0:
                    pe.wait_ge(trc_s, TR_AT["a", g] + GT)
                    if g:
                        pe.wait_ge(exp_s, g * GT)
                if n < 2:
                    for c in range(KC):
                        ins = pe.matmul(bank[3 + n][:, :], wqkv[:, c, n * HD:(n + 1) * HD], src[:, c, :], start=(c == 0), stop=(c == KC - 1))
                    ins.then_inc(qkv_s, 1)
                    return
                if g:
                    pe.wait_ge(qkvc_s, 3 * g)
                for i in range(GT):
                    for c in range(KC):
                        ins = pe.matmul(bank[5][:, i * P:(i + 1) * P], src[:, c, i * P:(i + 1) * P], wqkv[:, c, 2 * HD:3 * HD],
                                        start=(c == 0), stop=False)
                    ins = pe.matmul(bank[5][:, i * P:(i + 1) * P], sel_bv[:, :], b12[:, 0:HD], start=False, stop=True)
                ins.then_inc(qkv_s, 1)

            def scores(g, i):
                if i == 0:
                    pe.wait_ge(qkvc_s, 3 * g + 2)
                if i >= 2:
                    pe.wait_ge(exp_s, g * GT + i - 1)
                pe.matmul(bank[3 + i % 2][:, :], qT[:, i * P:(i + 1) * P], kT, start=True, stop=True).then_inc(sc_s, 1)

            def probs_T(g, i):
                k = TR_AT["p", g] + i
                pe.wait_ge(prob_s, g * GT + i + 1)
                pe.wait_ge(trc_s, k - 1)
                for t in range(GT):
                    ins = pe.transpose(bank[k % 2][:, t * P:(t + 1) * P], prob[:, i % 2, t * P:(t + 1) * P], ident)
                ins.then_inc(tr_s, 1)

            def pv(g, i):
                n = g * GT + i
                pe.wait_ge(trc_s, TR_AT["p", g] + i + 1)
                pe.wait_ge(qkvc_s, 3 * g + 3)
                if n:
                    pe.wait_ge(pvc_s, n)
                for t in range(GT):
                    ins = pe.matmul(bank[6][:, 0:P], v[:, t, :], pT[:, i % 2, t, :], start=(t == 0), stop=(t == GT - 1))
                ins.then_inc(pv_s, 1)

            def out_proj(g, i):
                n = g * GT + i
                pe.wait_ge(pvc_s, n + 1)
                if n:
                    pe.wait_ge(att_s, n)
                pe.matmul(bank[7][:, :], sel_bo[:, :], b3[:, :], start=True, stop=False)
                pe.matmul(bank[7][:, :], oT[:, i % 2, :], wo, start=False, stop=True).then_inc(o_s, 1)

            def softmax_part(g):
                scores(g, 0)
                scores(g, 1)
                probs_T(g, 0)
                for i in range(GT):
                    if i + 2 < GT:
                        scores(g, i + 2)
                    if i + 1 < GT:
                        probs_T(g, i + 1)
                    pv(g, i)
                    if i:
                        out_proj(g, i - 1)
                out_proj(g, GT - 1)

            def block_T(l, b, r):
                s = r % 2
                pe.wait_ge(got_s[r], ring_count(l, b, r) + 16)
                if not (l == 0 and isinstance(b, int) and b < 2):
                    pe.wait_ge(gTc_s, b + (l * NB - 1))
                for c in range(KC):
                    ins = pe.transpose(bank[s][:, c * P:(c + 1) * P], xg[:, r, c * P:(c + 1) * P], ident)
                ins.then_inc(gT_s, 1)

            def block_gate_up(l, b, s):
                e = pe.value_load(eid[0:1, bass.ds(b, 1)], min_val=0, max_val=E - 1)
                pe.wait_ge(gTc_s, b + (l * NB + 1))
                if not (l == 0 and isinstance(b, int) and b < 2):
                    pe.wait_ge(eh_s, b + (l * NB - 1))
                o = bank[3 + s][:, 0:2 * FI]
                pe.matmul(o, eoh[:, bass.ds(b, 1)].to_broadcast([P, P]), b12[:, :], start=True, stop=False)
                for c in range(KC):
                    ins = pe.matmul(o, xgT[:, s, c, :], w12[:, c, bass.ds(e * (2 * FI), 2 * FI)], start=False, stop=(c == KC - 1))
                ins.then_inc(egu_s, 1)

            def block_h_T(l, b, s):
                pe.wait_ge(eh_s, b + (l * NB + 1))
                if not (l == 0 and isinstance(b, int) and b == 0):
                    pe.wait_ge(ehTc_s, b + l * NB)
                pe.transpose(bank[5][:, 0:P], e_h[:, s, :], ident).then_inc(ehT_s, 1)

            def block_down(l, b, s):
                e = pe.value_load(eid[0:1, bass.ds(b, 1)], min_val=0, max_val=E - 1)
                pe.wait_ge(ehTc_s, b + (l * NB + 1))
                if not (l == 0 and isinstance(b, int) and b < 2):
                    pe.wait_ge(yo_s, b + (l * NB - 1))
                o = bank[6 + s][:, :]
                pe.matmul(o, eoh[:, bass.ds(b, 1)].to_broadcast([P, P]), b3[:, :], start=True, stop=False)
                pe.matmul(o, e_hT[:, s, :], w3[:, bass.ds(e * D, D)], start=False, stop=True).then_inc(ed_s, 1)

            def experts(l):
                pe.wait_ge(index_s, l + 1)
                if l == 0:
                    pe.wait_ge(w12_s, 16)
                    pe.wait_ge(w3_s, 16)
                block_T(l, 0, 0)
                block_gate_up(l, 0, 0)
                block_T(l, 1, 1)
                block_h_T(l, 0, 0)
                block_gate_up(l, 1, 1)
                block_T(l, 2, 2)
                pe.wait_ge(zc_s, NT * (l + 1))
                block_down(l, 0, 0)
                block_h_T(l, 1, 1)
                assert (NB - 3) % RING == 0
                with pe.Fori(0, (NB - 3) // RING) as n:
                    b = n * RING + 2
                    for u in range(RING):
                        block_gate_up(l, b + u, u % 2)
                        block_T(l, b + (u + 1), (u + 3) % RING)
                        block_down(l, b + (u - 1), (u + 1) % 2)
                        block_h_T(l, b + u, u % 2)
                block_gate_up(l, NB - 1, 0)
                block_down(l, NB - 2, 1)
                block_h_T(l, NB - 1, 0)
                block_down(l, NB - 1, 0)

            pe.wait_ge(keep_in_s, 16)
            pe.wait_ge(rw_s, 16)
            ffn_tiles(0, 0, range(GT), True)
            pe.wait_ge(sw12_s, 16)
            pe.wait_ge(sw3_s, 16)
            pe.wait_ge(consts_s, 1)
            shared_part(0, 0)
            for g in range(1, G):
                ffn_tiles(0, g, range(GT), True)
            shared_part(0, 1)
            prefix(0)
            shared_part(0, 2)
            table(0)
            shared_part(0, 3)
            experts(0)
            for i in range(GT):
                fill_T("a", 0, i)
            pe.wait_ge(attw_s, 32)
            for n in range(3):
                qkv(0, n)
            for i in range(GT):
                fill_T("a", 1, i)
            softmax_part(0)
            for g in range(1, G):
                last = g == G - 1
                qkv(g, 0)
                if not last:
                    ffn_tiles(1, g - 1, (0, 1))
                qkv(g, 1)
                if not last:
                    ffn_tiles(1, g - 1, (2, 3), True)
                qkv(g, 2)
                if last:
                    ffn_tiles(1, g - 1, range(GT), True)
                else:
                    for i in range(GT):
                        fill_T("a", g + 1, i)
                softmax_part(g)
            shared_part(1, 0)
            ffn_tiles(1, 3, range(GT), True)
            shared_part(1, 1)
            prefix(1)
            shared_part(1, 2)
            table(1)
            shared_part(1, 3)
            experts(1)

        @block.vector
        def _(ve):
            steps = [0]

            def settle(ins):
                steps[0] += 1
                ins.then_inc(vstep, 1)
                ve.wait_ge(vstep, steps[0])

            def kc(c, n):
                return keep[:, c:c + n]

            def combine(l, g):
                for i in range(GT):
                    t = g * GT + i
                    n = l * NT + t
                    ve.wait_ge(yin_s[i % 2], 16 * (n // 2 + 1))
                    if n % NT == 0:
                        ve.wait_ge(zadd_s, GT * G * (l + 1))
                    settle(ve.scalar_tensor_tensor(out=x[:, t, :], in0=yin[:, i % 2, 0, :], scalar=gates[:, 0, t:t + 1],
                                                   in1=x[:, t, :], op0=ALU.mult, op1=ALU.add))
                    ve.scalar_tensor_tensor(out=x[:, t, :], in0=yin[:, i % 2, 1, :], scalar=gates[:, 1, t:t + 1],
                                            in1=x[:, t, :], op0=ALU.mult, op1=ALU.add).then_inc(comb_s, 1)

            def norm(kind, g):
                n = LN_AT[kind, g] // GT
                if kind == "f0":
                    ve.wait_ge(x_s[g], 16)
                elif kind == "a":
                    combine(0, g)
                    ve.wait_ge(comb_s, (g + 1) * GT)
                for i in range(GT):
                    ins = ve.bn_stats(st6[:, i, :], x[:, g * GT + i, :])
                settle(ins)
                for i in range(GT):
                    ins = ve.bn_aggr(mv[:, i, :], st6[:, i, :])
                settle(ins)
                ve.tensor_scalar(veps[:, :], mv[:, :, 1], EPS, None, ALU.add).then_inc(var_s, 1)
                ve.wait_ge(rstd_s, n + 1)
                for i in range(GT):
                    j = LN_AT[kind, g] + i
                    if j >= 2:
                        before = LN_ORDER[(j - 2) // GT]
                        ve.wait_ge(tr_s, TR_AT[before] + (j - 2) % GT + 1)
                        if stores_before(kind, g, i):
                            ve.wait_ge(xn_out[i % 2], 16 * stores_before(kind, g, i))
                    ve.tensor_scalar(xn[:, i % 2, :], x[:, g * GT + i, :], mv[:, i, 0:1], rstd[:, i:i + 1], ALU.subtract,
                                     ALU.mult).then_inc(xn_s, 1)

            def attn(g):
                def row_max(i):
                    ve.wait_ge(sc_s, g * GT + i + 1)
                    settle(ve.tensor_reduce(rinv[:, i:i + 1], bank[3 + i % 2][:, :], AX.X, ALU.max))
                    ve.tensor_scalar(nmax[:, i:i + 1], rinv[:, i:i + 1], -SCALE, None, ALU.mult).then_inc(nmax_s, 1)

                def scale(i):
                    ve.wait_ge(exp_s, g * GT + i + 1)
                    settle(ve.reciprocal(rinv[:, i:i + 1], rsum[:, i:i + 1]))
                    ve.tensor_scalar(prob[:, i % 2, :], prob[:, i % 2, :], rinv[:, i:i + 1], None, ALU.mult).then_inc(prob_s, 1)

                def add(i):
                    t = g * GT + i
                    ve.wait_ge(o_s, t + 1)
                    ve.tensor_tensor(x[:, t, :], x[:, t, :], bank[7][:, :], ALU.add).then_inc(att_s, 1)

                row_max(0)
                row_max(1)
                scale(0)
                for i in range(GT):
                    if i + 2 < GT:
                        row_max(i + 2)
                    if i + 1 < GT:
                        scale(i + 1)
                    if i:
                        add(i - 1)
                add(GT - 1)
                ve.wait_ge(att_s, (g + 1) * GT)

            def first_max(out, vals, tmp, red, rev, shape):
                n = shape[-1]
                settle(ve.tensor_reduce(red, vals, AX.X, ALU.max))
                settle(ve.tensor_tensor(tmp, vals, red.unsqueeze(2).to_broadcast(shape), ALU.is_equal))
                settle(ve.tensor_tensor(tmp, tmp, rev, ALU.mult))
                settle(ve.tensor_reduce(red, tmp, AX.X, ALU.max))
                settle(ve.tensor_tensor(out, tmp, red.unsqueeze(2).to_broadcast(shape), ALU.is_equal))

            NE = NT * E
            A = [work[:, n * NE:(n + 1) * NE] for n in range(8)]
            te = lambda a: a.rearrange("p (t e) -> p t e", e=E)
            S3 = [P, NT, E]

            def route_choose(l):
                lg, tmp, sc, ms = A[0], A[1], A[2], A[3]
                oh = [A[4], A[5]]
                red = s16[:, 0:16]
                gm, gk, gt_, g1 = (A[6][:, 64 * n:64 * n + 64].rearrange("p (t j) -> p t j", j=EG) for n in range(4))
                ve.wait_ge(logit_s, (l + 1) * G)
                settle(ve.tensor_tensor(te(lg), te(bank[2][:, 0:NE]), kc(C_RB, E).unsqueeze(1).to_broadcast(S3), ALU.add))
                settle(ve.tensor_reduce(red, te(lg), AX.X, ALU.max))
                ve.tensor_tensor(te(lg), te(lg), red.unsqueeze(2).to_broadcast(S3), ALU.subtract).then_inc(lb_s, 1)
                ve.wait_ge(ex_s, l + 1)
                settle(ve.tensor_reduce(red, te(lg), AX.X, ALU.add))
                settle(ve.reciprocal(red, red))
                settle(ve.tensor_tensor(te(sc), te(lg), red.unsqueeze(2).to_broadcast(S3), ALU.mult))
                settle(ve.tensor_tensor(te(sc), te(sc), kc(C_RBIAS, E).unsqueeze(1).to_broadcast(S3), ALU.add))
                sh4 = [P, NT, EG]
                rev4 = kc(C_REV4, EG).unsqueeze(1).to_broadcast(sh4)
                settle(ve.tensor_reduce(gm.rearrange("p t j -> p (t j)"), sc.rearrange("p (a b) -> p a b", b=E // EG), AX.X, ALU.max))
                first_max(g1, gm, gt_, red, rev4, sh4)
                settle(ve.tensor_copy(gk, g1))
                settle(ve.scalar_tensor_tensor(out=gm, in0=g1, scalar=LOW, in1=gm, op0=ALU.mult, op1=ALU.add))
                first_max(g1, gm, gt_, red, rev4, sh4)
                settle(ve.tensor_tensor(gk, gk, g1, ALU.add))
                settle(ve.tensor_scalar(gk, gk, -1.0, -LOW, ALU.add, ALU.mult))
                s64 = [P, NT * EG, E // EG]
                settle(ve.tensor_tensor(ms.rearrange("p (a b) -> p a b", b=E // EG), sc.rearrange("p (a b) -> p a b", b=E // EG),
                                        gk.rearrange("p t j -> p (t j)").unsqueeze(2).to_broadcast(s64), ALU.add))
                rev16 = kc(C_REV16, E).unsqueeze(1).to_broadcast(S3)
                for k in range(TOPK):
                    first_max(te(oh[k]), te(ms), te(tmp), red, rev16, S3)
                    settle(ve.tensor_tensor(tmp, oh[k], sc, ALU.mult))
                    settle(ve.tensor_reduce(red, te(tmp), AX.X, ALU.add))
                    if k == 0:
                        settle(ve.scalar_tensor_tensor(out=ms, in0=oh[0], scalar=LOW, in1=ms, op0=ALU.mult, op1=ALU.add))
                    settle(ve.tensor_scalar(gates[:, k, :], red, 0.5, None, ALU.mult))
                chosen = work[:, 4480:4608].bitcast(BF16)
                ve.tensor_tensor(chosen, oh[0], oh[1], ALU.add).then_inc(chosen_s, 1)

            def route_slots(l):
                oh = [A[4], A[5]]
                tot = [work[:, 6 * NE + n * 384:6 * NE + (n + 1) * 384].rearrange("p (t e) -> p t e", e=E) for n in range(2)]
                PAD = 8
                cnt, nblk, start, tmp16, end = (s16[:, 16 * n:16 * n + 16] for n in range(1, 6))
                cmp = A[0].rearrange("p (a b) -> p a b", b=16)
                slot = te(A[1])
                ve.wait_ge(prefix_s, l + 1)
                ve.memset(tot[0][:, 0:PAD, :], 0.0)
                ve.memset(tot[1][:, 0:PAD, :], 0.0)
                settle(ve.tensor_copy(tot[0][:, PAD:, :], te(bank[1][:, 0:NE])))
                for n, d in enumerate((1, 2, 4, 8)):
                    a, b = tot[n % 2], tot[1 - n % 2]
                    settle(ve.tensor_tensor(b[:, PAD:, :], a[:, PAD:, :], a[:, PAD - d:PAD + NT - d, :], ALU.add))
                incl = tot[0]
                settle(ve.tensor_copy(cnt, incl[:, PAD + NT - 1, :]))
                sh = [P, E, 16]
                settle(ve.tensor_tensor(cmp, cnt.unsqueeze(2).to_broadcast(sh), kc(C_THR, 16).unsqueeze(1).to_broadcast(sh), ALU.is_gt))
                settle(ve.tensor_reduce(nblk, cmp, AX.X, ALU.add))
                settle(ve.tensor_tensor(cmp, kc(C_THR, 16).unsqueeze(2).to_broadcast(sh), kc(C_THR, 16).unsqueeze(1).to_broadcast(sh), ALU.is_gt))
                settle(ve.tensor_tensor(cmp, cmp, nblk.unsqueeze(1).to_broadcast(sh), ALU.mult))
                settle(ve.tensor_reduce(start, cmp, AX.X, ALU.add))
                settle(ve.tensor_tensor(end, start, nblk, ALU.add))
                settle(ve.tensor_scalar(start, start, float(P), None, ALU.mult))
                settle(ve.tensor_tensor(slot, te(bank[0][:, 0:NE]), incl[:, PAD - 1:PAD + NT - 1, :], ALU.add))
                settle(ve.tensor_tensor(slot, slot, start.unsqueeze(1).to_broadcast(S3), ALU.add))
                for k in range(TOPK):
                    settle(ve.tensor_tensor(te(A[2]), slot, te(oh[k]), ALU.mult))
                    settle(ve.tensor_reduce(slot_f[:, k * NT:(k + 1) * NT], te(A[2]), AX.X, ALU.add))
                settle(ve.tensor_copy(slot_i[:, :], slot_f[:, :]))
                settle(ve.tensor_scalar(r_i[:, :], slot_i[:, :], P - 1, None, ALU.bitwise_and))
                settle(ve.tensor_scalar(b_i[:, :], slot_i[:, :], 7, None, ALU.logical_shift_right))
                settle(ve.tensor_copy(r_f[:, :], r_i[:, :]))
                settle(ve.tensor_copy(b_f[:, :], b_i[:, :]))
                ecmp = work[:, 2048:2048 + NBP * E].rearrange("p (b e) -> p b e", e=E)
                she = [P, NBP, E]
                eb = work[:, 3072:3072 + NBP]
                settle(ve.tensor_tensor(ecmp, kc(C_B, NBP).unsqueeze(2).to_broadcast(she), end.unsqueeze(1).to_broadcast(she), ALU.is_ge))
                settle(ve.tensor_reduce(eb, ecmp, AX.X, ALU.add))
                settle(ve.tensor_scalar(eb, eb, float(E - 1), None, ALU.min))
                settle(ve.tensor_copy(eid[0:1, :], eb[0:1, :]))
                settle(ve.tensor_scalar(eoh[:, :], eb, keep[:, C_EMOD:C_EMOD + 1], None, ALU.is_equal))
                NK = TOPK * NT
                ohr = work[:, 0:2048].bitcast(BF16).rearrange("p (n r) -> p n r", r=P)
                obv = work[:, 2048:2048 + NBP * NK].bitcast(BF16).rearrange("p (n v b) -> p n v b", v=2, b=NBP)
                shb = [P, NK, NBP]
                settle(ve.tensor_tensor(ohr, kc(C_R, P).unsqueeze(1).to_broadcast([P, NK, P]), r_f[:, :].unsqueeze(2).to_broadcast([P, NK, P]), ALU.is_equal))
                ob = work[:, 3584:3584 + NBP * NK // 2].bitcast(BF16).rearrange("p (n b) -> p n b", b=NBP)
                settle(ve.tensor_tensor(ob, kc(C_B, NBP).unsqueeze(1).to_broadcast(shb), b_f[:, :].unsqueeze(2).to_broadcast(shb), ALU.is_equal))
                settle(ve.tensor_tensor(obv[:, :, 0, :], ob, kc(C_TK, NK).unsqueeze(2).to_broadcast(shb), ALU.mult))
                ve.tensor_scalar(obv[:, :, 1, :], ob, keep[:, C_P:C_P + 1], None, ALU.mult).then_inc(onehot_s, 1)

            def route_index(l):
                tk, pos, row, none = (work[:, 64 * n:64 * n + NBP] for n in range(4))
                ri = work[:, 256:256 + NBP].bitcast(I32)
                ni = work[:, 320:320 + NBP].bitcast(I32)
                ve.wait_ge(table_s, l + 1)
                settle(ve.tensor_copy(tk, bank[0][:, 0:NBP]))
                settle(ve.tensor_scalar(none, tk, 0.0, float(OUTSIDE), ALU.is_equal, ALU.mult))
                settle(ve.tensor_scalar(row, tk, -1.0, float(P), ALU.add, ALU.mult))
                settle(ve.tensor_tensor(row, row, bank[0][:, NBP:2 * NBP], ALU.add))
                settle(ve.tensor_scalar(row, row, 0.0, None, ALU.max))
                settle(ve.tensor_tensor(pos, row, none, ALU.add))
                settle(ve.tensor_copy(sidx[:, :], pos))
                settle(ve.tensor_scalar(pos, row, float(T), -float(T), ALU.is_ge, ALU.mult))
                settle(ve.tensor_tensor(row, row, pos, ALU.add))
                settle(ve.tensor_tensor(row, row, none, ALU.add))
                ve.tensor_copy(gidx[:, :], row).then_inc(index_s, 1)

            def block_h(l, b, s):
                ve.wait_ge(esilu_s, b + (l * NB + 1))
                ve.tensor_tensor(e_h[:, s, :], e_silu[:, s, :], bank[3 + s][:, FI:2 * FI], ALU.mult).then_inc(eh_s, 1)

            def block_hT(l, b, s):
                ve.wait_ge(ehT_s, b + (l * NB + 1))
                ve.tensor_copy(e_hT[:, s, :], bank[5][:, 0:P]).then_inc(ehTc_s, 1)

            def block_out(l, b, r):
                ve.wait_ge(ed_s, b + (l * NB + 1))
                if not (l == 0 and isinstance(b, int) and b < RING):
                    ve.wait_ge(put_s[r], ring_count(l, b, r))
                ve.tensor_copy(yo[:, r, :], bank[6 + r % 2][:, :]).then_inc(yo_s, 1)

            def experts(l):
                def step(b, r):
                    block_h(l, b, r % 2)
                    if not (isinstance(b, int) and b == 0):
                        block_out(l, b - 1, (r - 1) % RING)
                    block_hT(l, b, r % 2)

                first = 2 * RING - 1
                for b in range(first):
                    step(b, b % RING)
                assert (NB - first) % RING == 0
                with ve.Fori(0, (NB - first) // RING) as n:
                    b = n * RING + first
                    for u in range(RING):
                        step(b + u, (first + u) % RING)
                block_out(l, NB - 1, (NB - 1) % RING)

            norm("f0", 0)
            once = lambda c, n: work[:, c:c + n]
            ve.wait_ge(once_s, 16)
            ve.wait_ge(keep_in_s, 16)
            ve.tensor_copy(tri[:, :], once(S_TRI, P))
            ve.tensor_copy(sel_sb3[:, :], once(S_SELS, P))
            ve.tensor_copy(sel_bo[:, :], once(S_SELO, P))
            ve.tensor_copy(sel_bv[:, :], once(S_SELV, P))
            settle(ve.memset(ones[:, :], 1.0))
            raw = once(S_B12, 2 * FI + D)
            NR = 2 * FI + D
            hi = work[:, 2048:2048 + NR // 2].bitcast(BF16)
            mid = work[:, 2560:2560 + NR // 2].bitcast(BF16)
            acc = work[:, 3072:3072 + NR]
            settle(ve.tensor_copy(hi, raw))
            settle(ve.tensor_tensor(raw, raw, hi, ALU.subtract))
            settle(ve.tensor_copy(mid, raw))
            settle(ve.tensor_tensor(raw, raw, mid, ALU.subtract))
            m = [keep[:, C_MASK + n:C_MASK + n + 1] for n in range(3)]
            settle(ve.tensor_scalar(acc, hi, m[0], None, ALU.mult))
            settle(ve.scalar_tensor_tensor(out=acc, in0=mid, scalar=m[1], in1=acc, op0=ALU.mult, op1=ALU.add))
            settle(ve.scalar_tensor_tensor(out=acc, in0=raw, scalar=m[2], in1=acc, op0=ALU.mult, op1=ALU.add))
            settle(ve.tensor_copy(b12[:, :], acc[:, 0:2 * FI]))
            ve.tensor_copy(b3[:, :], acc[:, 2 * FI:NR]).then_inc(consts_s, 1)
            for g in range(1, G):
                norm("f0", g)
            route_choose(0)
            route_slots(0)
            route_index(0)
            experts(0)
            norm("a", 0)
            norm("a", 1)
            attn(0)
            for g in range(1, G):
                norm("f1", g - 1)
                if g + 1 < G:
                    norm("a", g + 1)
                attn(g)
            norm("f1", G - 1)
            route_choose(1)
            route_slots(1)
            route_index(1)
            experts(1)
            for g in range(G):
                combine(1, g)


def kernel(**inputs):
    import numpy as np
    import concourse.bacc as bacc
    from concourse.bass_utils import run_bass_kernel_spmd

    a = {k.removeprefix("L0_"): np.asarray(v, dtype=None) for k, v in inputs.items()}
    f32 = np.float32
    keep = np.zeros((P, NKEEP), f32)
    p = np.arange(P)
    keep[:, C_ID:C_ID + P] = np.eye(P, dtype=f32)
    keep[:, C_R:C_R + P] = np.arange(P)
    keep[:, C_B:C_B + NBP] = np.arange(NBP)
    keep[:, C_REV16:C_REV16 + 16] = 16 - np.arange(16)
    keep[:, C_REV4:C_REV4 + 4] = 4 - np.arange(4)
    keep[:, C_THR:C_THR + 16] = P * np.arange(16)
    keep[:, C_TK:C_TK + 32] = 1 + np.arange(32)
    keep[:, C_P] = p
    keep[:, C_EMOD] = np.where(p < 3 * E, p % E, -1)
    part = np.full(P, -1)
    part[:3 * E] = np.arange(3 * E) // E
    part[3 * E:3 * E + 9] = np.arange(9) % 3
    for n in range(3):
        keep[:, C_MASK + n] = part == n
    keep[:, C_SB1:C_SB1 + 2] = a["ffn_sb1"].reshape(SF, P).T
    keep[:, C_SB2:C_SB2 + 2] = a["ffn_sb2"].reshape(SF, P).T
    keep[:, C_BQKV:C_BQKV + 3] = a["attn_bqkv"].reshape(3, HD).T
    keep[:, C_RB:C_RB + E] = a["ffn_router_b"]
    keep[:, C_RBIAS:C_RBIAS + E] = a["ffn_router_bias"]
    once = np.zeros((P, NONCE), f32)
    once[:, S_TRI:S_TRI + P] = p[:, None] < p[None, :]
    once[3 * E:3 * E + 3, S_SELS:S_SELS + P] = 1
    once[3 * E + 3:3 * E + 6, S_SELO:S_SELO + P] = 1
    once[3 * E + 6:3 * E + 9, S_SELV:S_SELV + P] = 1
    for n in range(3):
        once[n * E:(n + 1) * E, S_B12:S_B12 + FI] = a["ffn_eb1"]
        once[n * E:(n + 1) * E, S_B12 + FI:S_B12 + 2 * FI] = a["ffn_eb2"]
        once[n * E:(n + 1) * E, S_B3:S_B3 + D] = a["ffn_eb3"]
    once[3 * E:3 * E + 3, S_B3:S_B3 + D] = a["ffn_sb3"]
    once[3 * E + 3:3 * E + 6, S_B3:S_B3 + D] = a["attn_bo"]
    once[3 * E + 6:3 * E + 9, S_B12:S_B12 + HD] = a["attn_bqkv"][2 * HD:]

    chunks = lambda w: w.reshape(-1, P, w.shape[-1]).transpose(1, 0, 2)
    both = np.stack([a["ffn_ew1"], a["ffn_ew2"]], axis=2)
    arrays = {
        "x_in": a["attn_x"].reshape(T, D),
        "keep_in": keep,
        "once_in": once,
        "rw_in": chunks(a["ffn_router_w"]),
        "w12_in": both.reshape(E, KC, P, 2 * FI).transpose(2, 1, 0, 3).reshape(P, KC, E * 2 * FI),
        "w3_in": a["ffn_ew3"].transpose(1, 0, 2).reshape(P, E * D),
        "sw12_in": chunks(np.concatenate([a["ffn_sw1"], a["ffn_sw2"]], axis=1)),
        "sw3_in": chunks(a["ffn_sw3"]),
        "wqkv_in": chunks(a["attn_Wqkv"]),
        "wo_in": a["attn_Wo"],
    }
    arrays = {k: np.ascontiguousarray(v) for k, v in arrays.items()}
    nc = bacc.Bacc("TRN2", target_bir_lowering=False, num_devices=1)
    ins = [nc.dram_tensor(k, v.shape, mybir.dt.from_np(v.dtype), kind="ExternalInput").ap() for k, v in arrays.items()]
    out = nc.dram_tensor("out", (T, D), mybir.dt.float32, kind="ExternalOutput").ap()
    macaron_kernel(nc, *ins, out)
    r = run_bass_kernel_spmd(nc, [arrays], core_ids=[0])
    return r.results[0]["out"].reshape(G, GW, D)
```

```python
import concourse.bass as bass
from concourse import mybir
from contextlib import ExitStack

P = 128
D = 512
KC = D // P
T = 2048
NT = T // P
G = 4
GT = NT // G
GW = GT * P
E = 16
EG = 4
TOPK = 2
FI = 128
SI = 256
SF = SI // P
HD = 128
EPS = 1e-5
SCALE = float(HD) ** -0.5
NB = (TOPK * T + E * (P - 1)) // P
NBP = NB + 1
RING = 4
LOW = -3.0e38
OUTSIDE = 1 << 20

C_ID, C_R, C_B = 0, 128, 256
C_REV16 = C_B + NBP
C_REV4 = C_REV16 + 16
C_THR = C_REV4 + 4
C_TK = C_THR + 16
C_P = C_TK + 32
C_EMOD = C_P + 1
C_MASK = C_EMOD + 1
C_SB1 = C_MASK + 3
C_SB2 = C_SB1 + 2
C_BQKV = C_SB2 + 2
C_RB = C_BQKV + 3
C_RBIAS = C_RB + 16
NKEEP = C_RBIAS + 16
S_TRI, S_SELS, S_SELV, S_B12, S_B3 = 0, 128, 256, 384, 640
NONCE = S_B3 + D


def macaron_kernel(nc, x_in, keep_in, once_in, rw_in, w12_in, w3_in, sw12_in, sw3_in, wqkv_in, wo_in, bo_in, out):
    F32, BF16, I32, U32 = mybir.dt.float32, mybir.dt.bfloat16, mybir.dt.int32, mybir.dt.uint32
    ALU, ACT, AX = mybir.AluOpType, mybir.ActivationFunctionType, mybir.AxisListType

    with ExitStack() as ctx:
        def sb(name, shape, dt=F32):
            return ctx.enter_context(nc.sbuf_tensor(name, shape, dt))

        def sem(name):
            return ctx.enter_context(nc.semaphore(name))

        bank = [ctx.enter_context(nc.psum_tensor(f"bank{i}", [P, 512], F32)) for i in range(8)]

        w12 = sb("w12", [P, KC, E * 2 * FI])
        w3 = sb("w3", [P, E * D])
        sw12 = sb("sw12", [P, KC, 2 * SI])
        sw3 = sb("sw3", [P, SF, D])
        rw = sb("rw", [P, KC, E])
        keep = sb("keep", [P, NKEEP])
        bo = sb("bo", [P, D])
        x = sb("x", [P, NT, D])
        b12 = sb("b12", [P, 2 * FI], BF16)
        b3 = sb("b3", [P, D], BF16)
        tri = sb("tri", [P, P], BF16)
        ones = sb("ones", [P, P], BF16)
        sel_sb3 = sb("sel_sb3", [P, P], BF16)
        sel_bv = sb("sel_bv", [P, P], BF16)
        eoh = sb("eoh", [P, NBP], BF16)
        gates = sb("gates", [P, TOPK, NT])
        EIDS = 3
        eid = sb("eid", [1, NBP + 4], I32)
        gidx = sb("gidx", [P, NBP], U32)
        sidx = sb("sidx", [P, NBP], U32)
        gi = sb("gi", [P, RING], U32)
        si = sb("si", [P, RING], U32)
        st6 = sb("st6", [P, 2, GT, 6])
        mv = sb("mv", [P, 3 * G, GT, 2])
        veps = sb("veps", [P, 3 * G, GT])
        rstd = sb("rstd", [P, 3 * G, GT])
        mhalf = sb("mhalf", [P, GT])
        nmax = sb("nmax", [P, GT])
        rsum = sb("rsum", [P, GT])
        rinv = sb("rinv", [P, GT])
        s16 = sb("s16", [P, 16 * 6])
        xn = sb("xn", [P, 2, D])
        xT = sb("xT", [P, 3, KC, GW])
        shared = sb("shared", [P, 4 * 512])
        work = sb("work", [P, 5888])

        sh_h = shared[:, 0:1024].rearrange("p (f n) -> p f n", f=SF)
        sh_u = shared[:, 1024:1536]
        wqkv = work[:, 0:1536].rearrange("p (c n) -> p c n", c=KC)
        wo = work[:, 1536:2048]
        qT, kT = work[:, 2048:2560], work[:, 2560:3072]
        v = work[:, 3072:3584].rearrange("p (t n) -> p t n", t=GT)
        prob = work[:, 3584:4608].rearrange("p (s n) -> p s n", s=2)
        pT = work[:, 4608:5632].rearrange("p (s t n) -> p s t n", s=2, t=GT)
        oT = work[:, 5632:5888].rearrange("p (s n) -> p s n", s=2)
        r32 = [work[:, 5632 + n * TOPK * NT:5632 + (n + 1) * TOPK * NT] for n in range(6)]
        slot_f, r_f, b_f = r32[0:3]
        slot_i, r_i, b_i = (a.bitcast(I32) for a in r32[3:6])
        sh_z = work[:, 4608:5632].rearrange("p (s n) -> p s n", s=2)
        ex1 = xT[:, 1, :, :].rearrange("p c n -> p (c n)")
        ex2 = xT[:, 2, :, :].rearrange("p c n -> p (c n)")
        xg = work[:, 2048:4096].rearrange("p (s n) -> p s n", s=RING)
        xgT = ex1[:, 0:1024].rearrange("p (s c n) -> p s c n", s=2, c=KC)
        yo = ex2[:, :].rearrange("p (s n) -> p s n", s=RING)
        e_silu = ex1[:, 1024:1280].rearrange("p (s n) -> p s n", s=2)
        e_h = ex1[:, 1280:1536].rearrange("p (s n) -> p s n", s=2)
        e_hT = ex1[:, 1536:1792].rearrange("p (s n) -> p s n", s=2)

        xn_slots = [xn[:, n, :] for n in range(2)] + [work[:, 2048 + n * D:2048 + (n + 1) * D] for n in range(5)]

        ident = keep[:, C_ID:C_ID + P]

        xn_d = [nc.dram_tensor(f"xn_d{l}", [T, D], F32) for l in range(2)]
        y_d = [nc.dram_tensor(f"y_d{l}", [TOPK * T, D], F32) for l in range(2)]

        keep_in_s, once_s, rw_s, x_s = sem("keep_loaded"), sem("once_loaded"), sem("rw_loaded"), [sem(f"x_loaded{g}") for g in range(G)]
        sw12_s, sw3_s, w12_s, w3_s = sem("sw12_loaded"), sem("sw3_loaded"), sem("w12_loaded"), sem("w3_loaded")
        attw_s, bo_in_s = sem("attn_weights_loaded"), sem("attn_bias_loaded")
        bo_s = sem("attn_bias_added")
        consts_s = sem("consts_ready")
        bn_s = sem("tile_stats_ready")
        mhalf_s = sem("mhalf_ready")
        vstep = sem("vector_step")
        var_s = sem("variance_ready")
        rstd_s = sem("rstd_ready")
        xn_s = sem("xn_ready")
        xn_out = [sem(f"xn_stored{n}") for n in range(7)]
        tr_s = sem("transposed")
        trc_s = sem("transposed_copied")
        logit_s = sem("logits_done")
        gu_s = sem("shared_gate_up_done")
        shact_s = sem("shared_act_done")
        shmul_s = sem("shared_mul_done")
        z_s = sem("shared_out_done")
        zc_s = sem("shared_out_copied")
        zadd_s = sem("shared_added")
        lb_s = sem("router_exp_in")
        ex_s = sem("router_exp_done")
        chosen_s = sem("chosen_ready")
        prefix_s = sem("prefix_done")
        onehot_s = sem("onehots_ready")
        table_s = sem("table_done")
        index_s = sem("indices_ready")
        gi_s, si_s = sem("gather_index"), sem("scatter_index")
        started_s = sem("indirect_dmas_started")
        got_s = [sem(f"gathered{s}") for s in range(RING)]
        put_s = [sem(f"scattered{s}") for s in range(RING)]
        gT_s, gTc_s = sem("block_transposed"), sem("block_transposed_copied")
        egu_s, esilu_s, eh_s = sem("block_gate_up"), sem("block_silu"), sem("block_h")
        ehT_s, ehTc_s = sem("block_h_transposed"), sem("block_h_transposed_copied")
        ed_s, yo_s = sem("block_down"), sem("block_out_ready")
        comb_s = sem("combined")
        qkv_s, qkvc_s = sem("qkv_done"), sem("qkv_copied")
        sc_s, nmax_s, exp_s = sem("scores_done"), sem("row_max_ready"), sem("exp_done")
        pv_s, pvc_s, o_s, att_s = sem("pv_done"), sem("pv_copied"), sem("attn_out_done"), sem("attn_added")
        out_s = sem("out_stored")

        LN_ORDER = [("f0", 0), ("f0", 1), ("f0", 2), ("f0", 3), ("a", 0), ("a", 1), ("f1", 0), ("a", 2), ("f1", 1),
                    ("a", 3), ("f1", 2), ("f1", 3)]
        LN_AT = {(*key, i): GT * n + i for n, key in enumerate(LN_ORDER) for i in range(GT)}

        def before_scores(g):
            return ("f1", g - 1) if 1 <= g < G - 1 else None

        def beside_softmax(g):
            return ("a", g + 1) if g < G - 1 else ("f1", G - 2)

        fills = [("f0", g, i) for g in range(G) for i in range(GT)] + [("a", 0, i) for i in range(GT)]
        for g in range(G):
            if before_scores(g):
                fills += [(*before_scores(g), i) for i in range(GT)]
            for i in range(GT):
                fills += [("p", g, i), (*beside_softmax(g), i)]
        fills += [("f1", G - 1, i) for i in range(GT)]
        TR_AT = {key: n for n, key in enumerate(fills)}
        LN_TILE = {n: key for key, n in LN_AT.items()}

        XN_AT = [j % len(xn_slots) if j < NT else j % 2 for j in range(GT * len(LN_ORDER))]

        def slot_before(j):
            return [n for n in range(j) if XN_AT[n] == XN_AT[j]]

        def stores_from(slot, tiles):
            return sum(XN_AT[n] == slot and LN_TILE[n][0] != "a" for n in tiles)

        BN_AT = {("f0", g): (g + 1) * GT for g in range(G)} | {("a", g): NT + (g + 1) * GT for g in range(2)}
        BN_AT |= {("f1", g): NT + 2 * GT + min(g + 1, 2) * GT + (g + 1) * GT for g in range(G)}
        BN_AT |= {("a", g + 2): BN_AT["f1", g] for g in range(2)}

        XT_SLOT = {("f0", g): g % 3 for g in range(G)} | {("a", g): 2 for g in range(G)} | {("f1", g): g % 3 for g in range(G)}
        share = lambda tiles, m: list(tiles)[m * len(tiles) // (2 * SF):(m + 1) * len(tiles) // (2 * SF)]
        SH = lambda l, g: l * G + g
        ring_base = lambda l, s: 16 * l * ((NB - s + RING - 1) // RING)
        ring_count = lambda l, b, s: b * (16 // RING) + (ring_base(l, s) - s * (16 // RING))

        places = [shared[:, n * 1024:(n + 1) * 1024] for n in range(2)] + [work[:, 3584 + n * 1024:4608 + n * 1024] for n in range(2)]
        places += [xT[:, n, :, :].rearrange("p c n -> p (c n)")[:, h * 1024:(h + 1) * 1024] for n in range(3) for h in range(2)]
        places += [work[:, n * 1024:(n + 1) * 1024] for n in range(3)]
        yin = [a.rearrange("p (k n) -> p k n", k=TOPK) for a in places]
        YIN_AT = [0, 1, 2, 3, 6, 7, 4, 5] + [0, 1, 6, 7] * 2 + [t % len(yin) for t in range(NT)]
        yin_s = [sem(f"results_loaded{n}") for n in range(len(yin))]
        yin_count = lambda n: 16 * YIN_AT[:n + 1].count(YIN_AT[n])

        block = ctx.enter_context(nc.Block())

        @block.sync
        def _(sp):
            def load_results(l, t):
                n = l * NT + t
                if t == 0:
                    for s in range(RING):
                        sp.wait_ge(put_s[s], ring_base(l + 1, s))
                    sp.wait_ge(zadd_s, NT * (l + 1))
                before = [m for m in range(n) if YIN_AT[m] == YIN_AT[n]]
                if before:
                    sp.wait_ge(comb_s, before[-1] + 1)
                yv = y_d[l].rearrange("(k t p) n -> t p k n", k=TOPK, p=P)
                sp.dma_start(yin[YIN_AT[n]], yv[t]).then_inc(yin_s[YIN_AT[n]], 16)

            xv = x_in.rearrange("(t p) n -> p t n", p=P)
            sp.dma_start(x[:, 0:GT, :], xv[:, 0:GT, :]).then_inc(x_s[0], 16)
            sp.dma_start(rw[:, :, :], rw_in).then_inc(rw_s, 16)
            sp.dma_start(sw12[:, :, :], sw12_in).then_inc(sw12_s, 16)
            sp.dma_start(work[:, 0:NONCE], once_in).then_inc(once_s, 16)
            sp.dma_start(x[:, GT:2 * GT, :], xv[:, GT:2 * GT, :]).then_inc(x_s[1], 16)
            sp.dma_start(sw3[:, :, :], sw3_in).then_inc(sw3_s, 16)
            sp.dma_start(bo[:, :], bo_in).then_inc(bo_in_s, 16)
            for g in range(2, G):
                sp.dma_start(x[:, g * GT:(g + 1) * GT, :], xv[:, g * GT:(g + 1) * GT, :]).then_inc(x_s[g], 16)
            sp.wait_ge(trc_s, NT)
            sp.dma_start(w12[:, :, :], w12_in).then_inc(w12_s, 16)
            sp.dma_start(w3[:, :], w3_in).then_inc(w3_s, 16)
            sp.wait_ge(index_s, 1)
            sp.dma_start(wqkv, wqkv_in).then_inc(attw_s, 16)
            sp.dma_start(wo, wo_in).then_inc(attw_s, 16)
            for l in range(2):
                for t in range(NT):
                    load_results(l, t)

        @block.gpsimd
        def _(pool):
            def rsqrt(n):
                pool.wait_ge(var_s, n + 1)
                pool.tensor_tensor(rstd[:, n, :], veps[:, n, :], mhalf[:, :], ALU.pow).then_inc(rstd_s, 1)

            def shared_part(l, g):
                u = SH(l, g)
                for f in range(SF):
                    pool.wait_ge(shact_s, u * 2 * SF + 2 * f + 2)
                    pool.tensor_tensor(sh_h[:, f, :], sh_h[:, f, :], sh_u, ALU.mult).then_inc(shmul_s, 1)
                if g == G - 1:
                    first_gathers(l)
                for i in range(GT):
                    t = g * GT + i
                    pool.wait_ge(zc_s, u * GT + i + 1)
                    pool.tensor_tensor(x[:, t, :], x[:, t, :], sh_z[:, i % 2, :], ALU.add).then_inc(zadd_s, 1)

            last_token, last_result = pool.to_reg(T - 1), pool.to_reg(TOPK * T - 1)

            def gather(l, b, s):
                pool.tensor_copy(gi[:, s:s + 1], gidx[:, bass.ds(b, 1)]).then_inc(gi_s, 1)
                pool.wait_ge(gi_s, b + (l * NB + 1))
                pool.sem_inc(started_s)
                pool.indirect_dma_start(xg[:, s, :], None, xn_d[l][:, :], bass.IndirectOffsetOnAxis(ap=gi[:, s:s + 1], axis=0),
                                        bounds_check=last_token, oob_is_err=False).then_inc(got_s[s], 16)

            def scatter(l, b, s):
                pool.wait_ge(yo_s, l * NB + b + 1)
                pool.tensor_copy(si[:, s:s + 1], sidx[:, bass.ds(b, 1)]).then_inc(si_s, 1)
                pool.wait_ge(si_s, b + (l * NB + 1))
                pool.sem_inc(started_s)
                pool.indirect_dma_start(y_d[l][:, :], bass.IndirectOffsetOnAxis(ap=si[:, s:s + 1], axis=0), yo[:, s, :], None,
                                        bounds_check=last_result, oob_is_err=False).then_inc(put_s[s], 16)

            def first_gathers(l):
                pool.wait_ge(index_s, l + 1)
                for s in range(len(xn_slots)):
                    pool.wait_ge(xn_out[s], 16 * stores_from(s, range(NT) if l == 0 else range(len(XN_AT))))
                for s in range(RING):
                    gather(l, s, s)

            def experts(l):
                whole = (NB - RING) // RING * RING
                with pool.Fori(0, whole, RING) as b:
                    for s in range(RING):
                        pool.wait_ge(gT_s, b + (l * NB + s + 1))
                        gather(l, b + (s + RING), s)
                        scatter(l, b + s, s)
                for b in range(whole, NB):
                    if b + RING < NB:
                        pool.wait_ge(gT_s, l * NB + b + 1)
                        gather(l, b + RING, b % RING)
                    scatter(l, b, b % RING)

            def attn_bias(g):
                for i in range(GT):
                    t = g * GT + i
                    pool.wait_ge(xn_s, LN_AT["a", g, i] + 1)
                    pool.tensor_tensor(x[:, t, :], x[:, t, :], bo[:, :], ALU.add).then_inc(bo_s, 1)

            pool.memset(mhalf[:, :], -0.5).then_inc(mhalf_s, 1)
            pool.wait_ge(mhalf_s, 1)
            for n in range(G):
                rsqrt(n)
            for g in range(G):
                shared_part(0, g)
            experts(0)
            pool.wait_ge(bo_in_s, 16)
            rsqrt(LN_ORDER.index(("a", 0)))
            rsqrt(LN_ORDER.index(("a", 1)))
            for g in range(G):
                attn_bias(g)
                rsqrt(LN_ORDER.index(("f1", g)))
                if g + 2 < G:
                    rsqrt(LN_ORDER.index(("a", g + 2)))
            for g in range(G):
                shared_part(1, g)
            experts(1)

        @block.scalar
        def _(act):
            def copy_T(kind, g, i):
                k = TR_AT[kind, g, i]
                act.wait_ge(tr_s, k + 1)
                if kind == "p":
                    dst = pT[:, i % 2, :, :]
                else:
                    dst = xT[:, XT_SLOT[kind, g], :, i * P:(i + 1) * P]
                if kind in ("f0", "f1"):
                    t = g * GT + i
                    slot = XN_AT[LN_AT[kind, g, i]]
                    act.dma_start(xn_d[int(kind[1])][t * P:(t + 1) * P, :], xn_slots[slot]).then_inc(xn_out[slot], 16)
                nc.scalar.activation(dst, bank[k % 2][:, :].rearrange("p (c n) -> p c n", c=KC), ACT.Copy).then_inc(trc_s, 1)

            def shared_part(l, g, beside_gate_up=(), beside_down=()):
                u = SH(l, g)
                beside_down = list(beside_down)
                for m in range(2 * SF):
                    act.wait_ge(gu_s, u * 2 * SF + m + 1)
                    f = m // 2
                    if m % 2 == 0:
                        if u:
                            act.wait_ge(z_s, u * GT)
                        nc.scalar.activation(sh_h[:, f, :], bank[3][:, :], ACT.Silu, bias=keep[:, C_SB1 + f:C_SB1 + f + 1]).then_inc(shact_s, 1)
                    else:
                        if u or f:
                            act.wait_ge(shmul_s, u * SF + f)
                        nc.scalar.activation(sh_u, bank[4][:, :], ACT.Identity, bias=keep[:, C_SB2 + f:C_SB2 + f + 1]).then_inc(shact_s, 1)
                    for tile in share(beside_gate_up, m):
                        copy_T(*tile)
                for i in range(GT):
                    n = u * GT + i
                    act.wait_ge(z_s, n + 1)
                    if n >= 2:
                        act.wait_ge(zadd_s, n - 1)
                    nc.scalar.activation(sh_z[:, i % 2, :], bank[6 + i % 2][:, :], ACT.Copy, scale=0.5).then_inc(zc_s, 1)
                    if beside_down:
                        copy_T(*beside_down.pop(0))

            def attn_copies(g, n):
                act.wait_ge(qkv_s, 3 * g + n + 1)
                if n < 2:
                    nc.scalar.activation([qT, kT][n], bank[3 + n][:, :], ACT.Identity, bias=keep[:, C_BQKV + n:C_BQKV + n + 1]).then_inc(qkvc_s, 1)
                else:
                    nc.scalar.activation(v, bank[5][:, :].rearrange("p (t n) -> p t n", t=GT), ACT.Copy).then_inc(qkvc_s, 1)

            def exp(g, i):
                act.wait_ge(nmax_s, g * GT + i + 1)
                nc.scalar.activation(prob[:, i % 2, :], bank[3 + i % 2][:, :], ACT.Exp, bias=nmax[:, i:i + 1], scale=SCALE,
                                     accum_out=rsum[:, i:i + 1]).then_inc(exp_s, 1)

            def copy_pv(g, i):
                n = g * GT + i
                act.wait_ge(pv_s, n + 1)
                nc.scalar.activation(oT[:, i % 2, :], bank[6][:, 0:P], ACT.Copy).then_inc(pvc_s, 1)

            def attention(g):
                attn_copies(g, 0)
                attn_copies(g, 1)
                if before_scores(g):
                    copy_T(*before_scores(g), 0)
                    copy_T(*before_scores(g), 1)
                exp(g, 0)
                exp(g, 1)
                if before_scores(g):
                    copy_T(*before_scores(g), 2)
                    copy_T(*before_scores(g), 3)
                attn_copies(g, 2)
                copy_T("p", g, 0)
                for i in range(GT):
                    copy_T(*beside_softmax(g), i)
                    if i + 1 < GT:
                        copy_T("p", g, i + 1)
                    if i + 2 < GT:
                        exp(g, i + 2)
                    copy_pv(g, i)

            def router_exp(l):
                act.wait_ge(lb_s, l + 1)
                nc.scalar.activation(work[:, 0:NT * E], work[:, 0:NT * E], ACT.Exp).then_inc(ex_s, 1)

            def block_act(l, b, s):
                q = l * NB + b
                act.wait_ge(egu_s, q + 1)
                nc.scalar.activation(e_silu[:, s, :], bank[3 + s][:, 0:FI], ACT.Silu).then_inc(esilu_s, 1)

            def block_copy_T(l, b, s):
                act.wait_ge(gT_s, b + (l * NB + 1))
                nc.scalar.activation(xgT[:, s, :, :], bank[s][:, :].rearrange("p (c n) -> p c n", c=KC), ACT.Copy).then_inc(gTc_s, 1)

            def experts(l):
                block_copy_T(l, 0, 0)
                with act.Fori(0, NB - 1, 2) as b:
                    for s in range(2):
                        block_act(l, b + s, s)
                        block_copy_T(l, b + (s + 1), 1 - s)
                block_act(l, NB - 1, 0)

            act.dma_start(keep[:, :], keep_in).then_inc(keep_in_s, 16)
            act.wait_ge(keep_in_s, 16)
            for i in range(GT):
                copy_T("f0", 0, i)
            shared_part(0, 0, [("f0", g, i) for g in (1, 2) for i in range(GT)], [("f0", 3, i) for i in range(GT)])
            router_exp(0)
            shared_part(0, 1)
            shared_part(0, 2)
            shared_part(0, 3)
            experts(0)
            for i in range(GT):
                copy_T("a", 0, i)
            for g in range(G):
                attention(g)
            shared_part(1, 0, (), [("f1", 3, i) for i in range(GT)])
            router_exp(1)
            for g in range(1, G):
                shared_part(1, g)
            experts(1)
            for t in range(NT):
                act.wait_ge(comb_s, NT + t + 1)
                act.dma_start(out[t * P:(t + 1) * P, :], x[:, t, :]).then_inc(out_s, 16)
            act.wait_ge(out_s, 16 * NT)

        @block.tensor
        def _(pe):
            def fill_T(kind, g, i):
                k = TR_AT[kind, g, i]
                pe.wait_ge(xn_s, LN_AT[kind, g, i] + 1)
                if k >= 2:
                    pe.wait_ge(trc_s, k - 1)
                for c in range(KC):
                    ins = pe.transpose(bank[k % 2][:, c * P:(c + 1) * P], xn_slots[XN_AT[LN_AT[kind, g, i]]][:, c * P:(c + 1) * P], ident)
                ins.then_inc(tr_s, 1)

            def router(l, g, i):
                kind = f"f{l}"
                t = g * GT + i
                pe.wait_ge(trc_s, TR_AT[kind, g, i] + 1)
                for c in range(KC):
                    ins = pe.matmul(bank[2][:, t * E:(t + 1) * E], xT[:, XT_SLOT[kind, g], c, i * P:(i + 1) * P], rw[:, c, :],
                                    start=(c == 0), stop=(c == KC - 1))
                ins.then_inc(logit_s, 1)

            waiting = []

            def fill(kind, g, i):
                fill_T(kind, g, i)
                flush()
                if kind != "a":
                    waiting.append((int(kind[1]), g, i))

            def flush():
                while waiting:
                    router(*waiting.pop())

            def shared_part(l, g, beside_gate_up=(), beside_down=()):
                u = SH(l, g)
                beside_down = list(beside_down)
                src = xT[:, XT_SLOT[f"f{l}", g], :, :]
                for m in range(2 * SF):
                    if u * 2 * SF + m >= 2:
                        pe.wait_ge(shact_s, u * 2 * SF + m - 1)
                    col = (m // 2) * P + (m % 2) * SI
                    for c in range(KC):
                        ins = pe.matmul(bank[3 + m % 2][:, :], sw12[:, c, col:col + P], src[:, c, :], start=(c == 0), stop=(c == KC - 1))
                    ins.then_inc(gu_s, 1)
                    for tile in share(beside_gate_up, m):
                        fill(*tile)

                def down(i, f):
                    n = u * GT + i
                    o = bank[6 + i % 2][:, :]
                    if f == 0:
                        pe.wait_ge(shmul_s, u * SF + 1)
                        if n >= 2:
                            pe.wait_ge(zc_s, n - 1)
                        if l and g == 0 and i == 1:
                            pe.wait_ge(att_s, NT)
                        pe.matmul(o, sel_sb3[:, :], b3[:, :], start=True, stop=False)
                    else:
                        pe.wait_ge(shmul_s, u * SF + 2)
                    ins = pe.matmul(o, sh_h[:, f, i * P:(i + 1) * P], sw3[:, f, :], start=False, stop=(f == SF - 1))
                    if f == SF - 1:
                        ins.then_inc(z_s, 1)
                        if beside_down:
                            fill(*beside_down.pop(0))

                if u == 0:
                    pe.wait_ge(sw3_s, 16)
                    pe.wait_ge(consts_s, 1)
                for i, f in ((0, 0), (1, 0), (0, 1), (1, 1), (2, 0), (2, 1), (3, 0), (3, 1)):
                    down(i, f)
                flush()

            def prefix(l):
                chosen = work[:, 4480:4608].bitcast(BF16)
                pe.wait_ge(chosen_s, l + 1)
                pe.matmul(bank[0][:, 0:NT * E], tri[:, :], chosen, start=True, stop=True)
                pe.matmul(bank[1][:, 0:NT * E], ones[:, :], chosen, start=True, stop=True).then_inc(prefix_s, 1)

            def table(l):
                ohr = work[:, 0:2048].bitcast(BF16)
                obv = work[:, 2048:2048 + 48 * 32].bitcast(BF16)
                pe.wait_ge(onehot_s, l + 1)
                for n in range(TOPK * NT):
                    ins = pe.matmul(bank[0][:, 0:2 * NBP], ohr[:, n * P:(n + 1) * P], obv[:, n * 2 * NBP:(n + 1) * 2 * NBP],
                                    start=(n == 0), stop=(n == TOPK * NT - 1))
                ins.then_inc(table_s, 1)

            def qkv(g, n):
                src = xT[:, XT_SLOT["a", g], :, :]
                if n == 0:
                    pe.wait_ge(trc_s, TR_AT["a", g, GT - 1] + 1)
                    if g:
                        pe.wait_ge(exp_s, g * GT)
                if n < 2:
                    for c in range(KC):
                        ins = pe.matmul(bank[3 + n][:, :], wqkv[:, c, n * HD:(n + 1) * HD], src[:, c, :], start=(c == 0), stop=(c == KC - 1))
                    ins.then_inc(qkv_s, 1)
                    return
                if g:
                    pe.wait_ge(qkvc_s, 3 * g)
                for i in range(GT):
                    for c in range(KC):
                        ins = pe.matmul(bank[5][:, i * P:(i + 1) * P], src[:, c, i * P:(i + 1) * P], wqkv[:, c, 2 * HD:3 * HD],
                                        start=(c == 0), stop=False)
                    ins = pe.matmul(bank[5][:, i * P:(i + 1) * P], sel_bv[:, :], b12[:, 0:HD], start=False, stop=True)
                ins.then_inc(qkv_s, 1)

            def scores(g, i):
                if i == 0:
                    pe.wait_ge(qkvc_s, 3 * g + 2)
                if i >= 2:
                    pe.wait_ge(exp_s, g * GT + i - 1)
                pe.matmul(bank[3 + i % 2][:, :], qT[:, i * P:(i + 1) * P], kT, start=True, stop=True).then_inc(sc_s, 1)

            def probs_T(g, i):
                k = TR_AT["p", g, i]
                pe.wait_ge(exp_s, g * GT + i + 1)
                pe.wait_ge(trc_s, k - 1)
                for t in range(GT):
                    ins = pe.transpose(bank[k % 2][:, t * P:(t + 1) * P], prob[:, i % 2, t * P:(t + 1) * P], ident)
                ins.then_inc(tr_s, 1)

            def pv(g, i):
                n = g * GT + i
                pe.wait_ge(trc_s, TR_AT["p", g, i] + 1)
                pe.wait_ge(qkvc_s, 3 * g + 3)
                if n:
                    pe.wait_ge(pvc_s, n)
                for t in range(GT):
                    ins = pe.matmul(bank[6][:, 0:P], v[:, t, :], pT[:, i % 2, t, :], start=(t == 0), stop=(t == GT - 1))
                ins.then_inc(pv_s, 1)

            def out_proj(g, i):
                n = g * GT + i
                pe.wait_ge(pvc_s, n + 1)
                if n:
                    pe.wait_ge(att_s, n)
                pe.matmul(bank[7][:, :], oT[:, i % 2, :], wo, start=True, stop=True).then_inc(o_s, 1)

            def attention(g):
                qkv(g, 0)
                qkv(g, 1)
                if before_scores(g):
                    fill(*before_scores(g), 0)
                    fill(*before_scores(g), 1)
                scores(g, 0)
                scores(g, 1)
                if before_scores(g):
                    fill(*before_scores(g), 2)
                    fill(*before_scores(g), 3)
                qkv(g, 2)
                flush()
                probs_T(g, 0)
                for i in range(GT):
                    if i + 2 < GT:
                        scores(g, i + 2)
                    fill(*beside_softmax(g), i)
                    if i + 1 < GT:
                        probs_T(g, i + 1)
                    pv(g, i)
                    if i:
                        out_proj(g, i - 1)
                out_proj(g, GT - 1)
                flush()

            def block_T(l, b, r):
                s = r % 2
                pe.wait_ge(got_s[r], ring_count(l, b, r) + 16)
                if not (l == 0 and isinstance(b, int) and b < 2):
                    pe.wait_ge(gTc_s, b + (l * NB - 1))
                for c in range(KC):
                    ins = pe.transpose(bank[s][:, c * P:(c + 1) * P], xg[:, r, c * P:(c + 1) * P], ident)
                ins.then_inc(gT_s, 1)

            def experts_of(b, n):
                _, ids = nc.values_load_multi_w_load_instructions(eid[0:1, bass.ds(b + EIDS, n)], engines=(mybir.EngineType.PE,),
                                                                  min_val=0, max_val=E - 1)
                return ids

            def block_gate_up(l, b, s, e):
                pe.wait_ge(gTc_s, b + (l * NB + 1))
                if not (l == 0 and isinstance(b, int) and b < 2):
                    pe.wait_ge(eh_s, b + (l * NB - 1))
                o = bank[3 + s][:, 0:2 * FI]
                pe.matmul(o, eoh[:, bass.ds(b, 1)].to_broadcast([P, P]), b12[:, :], start=True, stop=False)
                for c in range(KC):
                    ins = pe.matmul(o, xgT[:, s, c, :], w12[:, c, bass.ds(e * (2 * FI), 2 * FI)], start=False, stop=(c == KC - 1))
                ins.then_inc(egu_s, 1)

            def block_h_T(l, b, s):
                pe.wait_ge(eh_s, b + (l * NB + 1))
                if not (l == 0 and isinstance(b, int) and b == 0):
                    pe.wait_ge(ehTc_s, b + l * NB)
                pe.transpose(bank[5][:, 0:P], e_h[:, s, :], ident).then_inc(ehT_s, 1)

            def block_down(l, b, s, e):
                pe.wait_ge(ehTc_s, b + (l * NB + 1))
                if not (l == 0 and isinstance(b, int) and b < 2):
                    pe.wait_ge(yo_s, b + (l * NB - 1))
                o = bank[6 + s][:, :]
                pe.matmul(o, eoh[:, bass.ds(b, 1)].to_broadcast([P, P]), b3[:, :], start=True, stop=False)
                pe.matmul(o, e_hT[:, s, :], w3[:, bass.ds(e * D, D)], start=False, stop=True).then_inc(ed_s, 1)

            def experts(l):
                pe.wait_ge(index_s, l + 1)
                if l == 0:
                    pe.wait_ge(w12_s, 16)
                    pe.wait_ge(w3_s, 16)
                block_T(l, 0, 0)
                def step(b, s, r, e, e_before):
                    block_gate_up(l, b, s, e)
                    if not (isinstance(b, int) and b == NB - 1):
                        block_T(l, b + 1, r)
                    if e_before is not None:
                        block_down(l, b - 1, 1 - s, e_before)
                    block_h_T(l, b, s)

                turn = 3 * RING
                first = (NB - 1) % turn
                ids = experts_of(0, first)
                step(0, 0, 1, ids[0], None)
                pe.wait_ge(zc_s, NT * (l + 1))
                for b in range(1, first):
                    step(b, b % 2, (b + 1) % RING, ids[b], ids[b - 1])
                with pe.Fori(0, (NB - 1) // turn) as n:
                    b = n * turn + first
                    ids = experts_of(b - 1, turn + 1)
                    for u in range(turn):
                        step(b + u, (first + u) % 2, (first + u + 1) % RING, ids[u + 1], ids[u])
                ids = experts_of(NB - 2, 2)
                step(NB - 1, 0, None, ids[1], ids[0])
                block_down(l, NB - 1, 0, ids[1])

            pe.wait_ge(keep_in_s, 16)
            pe.wait_ge(rw_s, 16)
            for i in range(GT):
                fill("f0", 0, i)
            flush()
            pe.wait_ge(sw12_s, 16)
            shared_part(0, 0, [("f0", g, i) for g in (1, 2) for i in range(GT)], [("f0", 3, i) for i in range(GT)])
            shared_part(0, 1)
            prefix(0)
            shared_part(0, 2)
            table(0)
            shared_part(0, 3)
            experts(0)
            for i in range(GT):
                fill("a", 0, i)
            pe.wait_ge(attw_s, 32)
            for g in range(G):
                attention(g)
            shared_part(1, 0, (), [("f1", 3, i) for i in range(GT)])
            shared_part(1, 1)
            prefix(1)
            shared_part(1, 2)
            table(1)
            shared_part(1, 3)
            experts(1)

        @block.vector
        def _(ve):
            steps = [0]

            def settle(ins):
                steps[0] += 1
                ins.then_inc(vstep, 1)
                ve.wait_ge(vstep, steps[0])

            def kc(c, n):
                return keep[:, c:c + n]

            def combine(l, t):
                n = l * NT + t
                ve.wait_ge(yin_s[YIN_AT[n]], yin_count(n))
                y = yin[YIN_AT[n]]
                settle(ve.scalar_tensor_tensor(out=x[:, t, :], in0=y[:, 0, :], scalar=gates[:, 0, t:t + 1],
                                               in1=x[:, t, :], op0=ALU.mult, op1=ALU.add))
                ve.scalar_tensor_tensor(out=x[:, t, :], in0=y[:, 1, :], scalar=gates[:, 1, t:t + 1],
                                        in1=x[:, t, :], op0=ALU.mult, op1=ALU.add).then_inc(comb_s, 1)

            def tile_stats(kind, g, i):
                if kind == "f0":
                    ve.wait_ge(x_s[g], 16)
                elif kind == "a":
                    ve.wait_ge(comb_s, g * GT + i + 1)
                else:
                    ve.wait_ge(att_s, g * GT + i + 1)
                ve.bn_stats(st6[:, kind == "a", i, :], x[:, g * GT + i, :]).then_inc(bn_s, 1)

            def group_stats(kind, g):
                n = LN_ORDER.index((kind, g))
                ve.wait_ge(bn_s, BN_AT[kind, g])
                for i in range(GT):
                    ins = ve.bn_aggr(mv[:, n, i, :], st6[:, kind == "a", i, :])
                settle(ins)
                ve.tensor_scalar(veps[:, n, :], mv[:, n, :, 1], EPS, None, ALU.add).then_inc(var_s, 1)

            def stats(kind, g):
                for i in range(GT):
                    tile_stats(kind, g, i)
                group_stats(kind, g)

            def normalize(kind, g, i):
                n = LN_ORDER.index((kind, g))
                j = LN_AT[kind, g, i]
                if i == 0:
                    ve.wait_ge(rstd_s, n + 1)
                if slot_before(j):
                    ve.wait_ge(tr_s, TR_AT[LN_TILE[slot_before(j)[-1]]] + 1)
                    ve.wait_ge(xn_out[XN_AT[j]], 16 * stores_from(XN_AT[j], range(j)))
                ve.tensor_scalar(xn_slots[XN_AT[j]], x[:, g * GT + i, :], mv[:, n, i, 0:1], rstd[:, n, i:i + 1], ALU.subtract,
                                 ALU.mult).then_inc(xn_s, 1)

            def attention(g):
                def row_max(i):
                    ve.wait_ge(sc_s, g * GT + i + 1)
                    settle(ve.tensor_reduce(nmax[:, i:i + 1], bank[3 + i % 2][:, :], AX.X, ALU.max))
                    ve.tensor_scalar(nmax[:, i:i + 1], nmax[:, i:i + 1], -SCALE, None, ALU.mult).then_inc(nmax_s, 1)

                def add(i):
                    t = g * GT + i
                    ve.wait_ge(exp_s, t + 1)
                    settle(ve.reciprocal(rinv[:, i:i + 1], rsum[:, i:i + 1]))
                    ve.wait_ge(o_s, t + 1)
                    ve.wait_ge(bo_s, t + 1)
                    ve.scalar_tensor_tensor(out=x[:, t, :], in0=bank[7][:, :], scalar=rinv[:, i:i + 1], in1=x[:, t, :],
                                            op0=ALU.mult, op1=ALU.add).then_inc(att_s, 1)

                if before_scores(g):
                    normalize(*before_scores(g), 0)
                    normalize(*before_scores(g), 1)
                row_max(0)
                row_max(1)
                if before_scores(g):
                    normalize(*before_scores(g), 2)
                    normalize(*before_scores(g), 3)
                normalize(*beside_softmax(g), 0)
                for i in range(GT):
                    if i + 2 < GT:
                        row_max(i + 2)
                    if i + 1 < GT:
                        normalize(*beside_softmax(g), i + 1)
                    if g + 2 < G:
                        combine(0, (g + 2) * GT + i)
                        tile_stats("a", g + 2, i)
                    if i:
                        add(i - 1)
                        tile_stats("f1", g, i - 1)
                add(GT - 1)
                tile_stats("f1", g, GT - 1)
                group_stats("f1", g)
                if g + 2 < G:
                    group_stats("a", g + 2)

            def first_max(out, vals, tmp, red, rev, shape):
                n = shape[-1]
                settle(ve.tensor_reduce(red, vals, AX.X, ALU.max))
                settle(ve.tensor_tensor(tmp, vals, red.unsqueeze(2).to_broadcast(shape), ALU.is_equal))
                settle(ve.tensor_tensor(tmp, tmp, rev, ALU.mult))
                settle(ve.tensor_reduce(red, tmp, AX.X, ALU.max))
                settle(ve.tensor_tensor(out, tmp, red.unsqueeze(2).to_broadcast(shape), ALU.is_equal))

            NE = NT * E
            A = [work[:, n * NE:(n + 1) * NE] for n in range(8)]
            te = lambda a: a.rearrange("p (t e) -> p t e", e=E)
            S3 = [P, NT, E]

            def route_choose(l):
                lg, tmp, sc, ms = A[0], A[1], A[2], A[3]
                oh = [A[4], A[5]]
                red = s16[:, 0:16]
                gm, gk, gt_, g1 = (A[6][:, 64 * n:64 * n + 64].rearrange("p (t j) -> p t j", j=EG) for n in range(4))
                ve.wait_ge(logit_s, (l + 1) * NT)
                settle(ve.tensor_tensor(te(lg), te(bank[2][:, 0:NE]), kc(C_RB, E).unsqueeze(1).to_broadcast(S3), ALU.add))
                settle(ve.tensor_reduce(red, te(lg), AX.X, ALU.max))
                ve.tensor_tensor(te(lg), te(lg), red.unsqueeze(2).to_broadcast(S3), ALU.subtract).then_inc(lb_s, 1)
                ve.wait_ge(ex_s, l + 1)
                settle(ve.tensor_reduce(red, te(lg), AX.X, ALU.add))
                settle(ve.reciprocal(red, red))
                settle(ve.tensor_tensor(te(sc), te(lg), red.unsqueeze(2).to_broadcast(S3), ALU.mult))
                settle(ve.tensor_tensor(te(sc), te(sc), kc(C_RBIAS, E).unsqueeze(1).to_broadcast(S3), ALU.add))
                sh4 = [P, NT, EG]
                rev4 = kc(C_REV4, EG).unsqueeze(1).to_broadcast(sh4)
                settle(ve.tensor_reduce(gm.rearrange("p t j -> p (t j)"), sc.rearrange("p (a b) -> p a b", b=E // EG), AX.X, ALU.max))
                first_max(g1, gm, gt_, red, rev4, sh4)
                settle(ve.tensor_copy(gk, g1))
                settle(ve.scalar_tensor_tensor(out=gm, in0=g1, scalar=LOW, in1=gm, op0=ALU.mult, op1=ALU.add))
                first_max(g1, gm, gt_, red, rev4, sh4)
                settle(ve.tensor_tensor(gk, gk, g1, ALU.add))
                settle(ve.tensor_scalar(gk, gk, -1.0, -LOW, ALU.add, ALU.mult))
                s64 = [P, NT * EG, E // EG]
                settle(ve.tensor_tensor(ms.rearrange("p (a b) -> p a b", b=E // EG), sc.rearrange("p (a b) -> p a b", b=E // EG),
                                        gk.rearrange("p t j -> p (t j)").unsqueeze(2).to_broadcast(s64), ALU.add))
                rev16 = kc(C_REV16, E).unsqueeze(1).to_broadcast(S3)
                for k in range(TOPK):
                    first_max(te(oh[k]), te(ms), te(tmp), red, rev16, S3)
                    settle(ve.tensor_tensor(tmp, oh[k], sc, ALU.mult))
                    settle(ve.tensor_reduce(red, te(tmp), AX.X, ALU.add))
                    if k == 0:
                        settle(ve.scalar_tensor_tensor(out=ms, in0=oh[0], scalar=LOW, in1=ms, op0=ALU.mult, op1=ALU.add))
                    settle(ve.tensor_scalar(gates[:, k, :], red, 0.5, None, ALU.mult))
                chosen = work[:, 4480:4608].bitcast(BF16)
                ve.tensor_tensor(chosen, oh[0], oh[1], ALU.add).then_inc(chosen_s, 1)

            def route_slots(l):
                oh = [A[4], A[5]]
                tot = [work[:, 6 * NE + n * 384:6 * NE + (n + 1) * 384].rearrange("p (t e) -> p t e", e=E) for n in range(2)]
                PAD = 8
                cnt, nblk, start, tmp16, end = (s16[:, 16 * n:16 * n + 16] for n in range(1, 6))
                cmp = A[0].rearrange("p (a b) -> p a b", b=16)
                slot = te(A[1])
                ve.wait_ge(prefix_s, l + 1)
                ve.memset(tot[0][:, 0:PAD, :], 0.0)
                ve.memset(tot[1][:, 0:PAD, :], 0.0)
                settle(ve.tensor_copy(tot[0][:, PAD:, :], te(bank[1][:, 0:NE])))
                for n, d in enumerate((1, 2, 4, 8)):
                    a, b = tot[n % 2], tot[1 - n % 2]
                    settle(ve.tensor_tensor(b[:, PAD:, :], a[:, PAD:, :], a[:, PAD - d:PAD + NT - d, :], ALU.add))
                incl = tot[0]
                settle(ve.tensor_copy(cnt, incl[:, PAD + NT - 1, :]))
                sh = [P, E, 16]
                settle(ve.tensor_tensor(cmp, cnt.unsqueeze(2).to_broadcast(sh), kc(C_THR, 16).unsqueeze(1).to_broadcast(sh), ALU.is_gt))
                settle(ve.tensor_reduce(nblk, cmp, AX.X, ALU.add))
                settle(ve.tensor_tensor(cmp, kc(C_THR, 16).unsqueeze(2).to_broadcast(sh), kc(C_THR, 16).unsqueeze(1).to_broadcast(sh), ALU.is_gt))
                settle(ve.tensor_tensor(cmp, cmp, nblk.unsqueeze(1).to_broadcast(sh), ALU.mult))
                settle(ve.tensor_reduce(start, cmp, AX.X, ALU.add))
                settle(ve.tensor_tensor(end, start, nblk, ALU.add))
                settle(ve.tensor_scalar(start, start, float(P), None, ALU.mult))
                settle(ve.tensor_tensor(slot, te(bank[0][:, 0:NE]), incl[:, PAD - 1:PAD + NT - 1, :], ALU.add))
                settle(ve.tensor_tensor(slot, slot, start.unsqueeze(1).to_broadcast(S3), ALU.add))
                for k in range(TOPK):
                    settle(ve.tensor_tensor(te(A[2]), slot, te(oh[k]), ALU.mult))
                    settle(ve.tensor_reduce(slot_f[:, k * NT:(k + 1) * NT], te(A[2]), AX.X, ALU.add))
                settle(ve.tensor_copy(slot_i[:, :], slot_f[:, :]))
                settle(ve.tensor_scalar(r_i[:, :], slot_i[:, :], P - 1, None, ALU.bitwise_and))
                settle(ve.tensor_scalar(b_i[:, :], slot_i[:, :], 7, None, ALU.logical_shift_right))
                settle(ve.tensor_copy(r_f[:, :], r_i[:, :]))
                settle(ve.tensor_copy(b_f[:, :], b_i[:, :]))
                ecmp = work[:, 2048:2048 + NBP * E].rearrange("p (b e) -> p b e", e=E)
                she = [P, NBP, E]
                eb = work[:, 3072:3072 + NBP]
                settle(ve.tensor_tensor(ecmp, kc(C_B, NBP).unsqueeze(2).to_broadcast(she), end.unsqueeze(1).to_broadcast(she), ALU.is_ge))
                settle(ve.tensor_reduce(eb, ecmp, AX.X, ALU.add))
                settle(ve.tensor_scalar(eb, eb, float(E - 1), None, ALU.min))
                settle(ve.tensor_copy(eid[0:1, EIDS:EIDS + NBP], eb[0:1, :]))
                settle(ve.tensor_scalar(eoh[:, :], eb, keep[:, C_EMOD:C_EMOD + 1], None, ALU.is_equal))
                NK = TOPK * NT
                ohr = work[:, 0:2048].bitcast(BF16).rearrange("p (n r) -> p n r", r=P)
                obv = work[:, 2048:2048 + NBP * NK].bitcast(BF16).rearrange("p (n v b) -> p n v b", v=2, b=NBP)
                shb = [P, NK, NBP]
                settle(ve.tensor_tensor(ohr, kc(C_R, P).unsqueeze(1).to_broadcast([P, NK, P]), r_f[:, :].unsqueeze(2).to_broadcast([P, NK, P]), ALU.is_equal))
                ob = work[:, 3584:3584 + NBP * NK // 2].bitcast(BF16).rearrange("p (n b) -> p n b", b=NBP)
                settle(ve.tensor_tensor(ob, kc(C_B, NBP).unsqueeze(1).to_broadcast(shb), b_f[:, :].unsqueeze(2).to_broadcast(shb), ALU.is_equal))
                settle(ve.tensor_tensor(obv[:, :, 0, :], ob, kc(C_TK, NK).unsqueeze(2).to_broadcast(shb), ALU.mult))
                ve.tensor_scalar(obv[:, :, 1, :], ob, keep[:, C_P:C_P + 1], None, ALU.mult).then_inc(onehot_s, 1)

            def route_index(l):
                tk, pos, row, none = (work[:, 64 * n:64 * n + NBP] for n in range(4))
                ri = work[:, 256:256 + NBP].bitcast(I32)
                ni = work[:, 320:320 + NBP].bitcast(I32)
                ve.wait_ge(table_s, l + 1)
                settle(ve.tensor_copy(tk, bank[0][:, 0:NBP]))
                settle(ve.tensor_scalar(none, tk, 0.0, float(OUTSIDE), ALU.is_equal, ALU.mult))
                settle(ve.tensor_scalar(row, tk, -1.0, float(P), ALU.add, ALU.mult))
                settle(ve.tensor_tensor(row, row, bank[0][:, NBP:2 * NBP], ALU.add))
                settle(ve.tensor_scalar(row, row, 0.0, None, ALU.max))
                settle(ve.tensor_tensor(pos, row, none, ALU.add))
                settle(ve.tensor_copy(sidx[:, :], pos))
                settle(ve.tensor_scalar(pos, row, float(T), -float(T), ALU.is_ge, ALU.mult))
                settle(ve.tensor_tensor(row, row, pos, ALU.add))
                settle(ve.tensor_tensor(row, row, none, ALU.add))
                ve.tensor_copy(gidx[:, :], row).then_inc(index_s, 1)

            def block_h(l, b, s):
                ve.wait_ge(esilu_s, b + (l * NB + 1))
                ve.tensor_tensor(e_h[:, s, :], e_silu[:, s, :], bank[3 + s][:, FI:2 * FI], ALU.mult).then_inc(eh_s, 1)

            def block_hT(l, b, s):
                ve.wait_ge(ehT_s, b + (l * NB + 1))
                ve.tensor_copy(e_hT[:, s, :], bank[5][:, 0:P]).then_inc(ehTc_s, 1)

            def block_out(l, b, r):
                ve.wait_ge(ed_s, b + (l * NB + 1))
                if not (l == 0 and isinstance(b, int) and b < RING):
                    ve.wait_ge(put_s[r], ring_count(l, b, r))
                ve.tensor_copy(yo[:, r, :], bank[6 + r % 2][:, :]).then_inc(yo_s, 1)

            def experts(l):
                def step(b, r):
                    block_h(l, b, r % 2)
                    if not (isinstance(b, int) and b == 0):
                        block_out(l, b - 1, (r - 1) % RING)
                    block_hT(l, b, r % 2)

                first = 2 * RING - 1
                for b in range(first):
                    step(b, b % RING)
                assert (NB - first) % RING == 0
                with ve.Fori(0, (NB - first) // RING) as n:
                    b = n * RING + first
                    for u in range(RING):
                        step(b + u, (first + u) % RING)
                block_out(l, NB - 1, (NB - 1) % RING)

            stats("f0", 0)
            for i in range(GT):
                normalize("f0", 0, i)
            once = lambda c, n: work[:, c:c + n]
            ve.wait_ge(once_s, 16)
            ve.wait_ge(keep_in_s, 16)
            ve.tensor_copy(tri[:, :], once(S_TRI, P))
            ve.tensor_copy(sel_sb3[:, :], once(S_SELS, P))
            ve.tensor_copy(sel_bv[:, :], once(S_SELV, P))
            settle(ve.memset(ones[:, :], 1.0))
            raw = once(S_B12, 2 * FI + D)
            NR = 2 * FI + D
            hi = work[:, 4608:4608 + NR // 2].bitcast(BF16)
            mid = work[:, 5120:5120 + NR // 2].bitcast(BF16)
            acc = work[:, 1280:1280 + NR]
            settle(ve.tensor_copy(hi, raw))
            settle(ve.tensor_tensor(raw, raw, hi, ALU.subtract))
            settle(ve.tensor_copy(mid, raw))
            settle(ve.tensor_tensor(raw, raw, mid, ALU.subtract))
            m = [keep[:, C_MASK + n:C_MASK + n + 1] for n in range(3)]
            settle(ve.tensor_scalar(acc, hi, m[0], None, ALU.mult))
            settle(ve.scalar_tensor_tensor(out=acc, in0=mid, scalar=m[1], in1=acc, op0=ALU.mult, op1=ALU.add))
            settle(ve.scalar_tensor_tensor(out=acc, in0=raw, scalar=m[2], in1=acc, op0=ALU.mult, op1=ALU.add))
            settle(ve.tensor_copy(b12[:, :], acc[:, 0:2 * FI]))
            ve.tensor_copy(b3[:, :], acc[:, 2 * FI:NR]).then_inc(consts_s, 1)
            for g in range(1, G):
                stats("f0", g)
                for i in range(GT):
                    normalize("f0", g, i)
            for s in range(2, len(xn_slots)):
                ve.wait_ge(xn_out[s], 16 * stores_from(s, range(NT)))
            route_choose(0)
            route_slots(0)
            route_index(0)
            experts(0)
            for i in range(GT):
                combine(0, i)
                tile_stats("a", 0, i)
            group_stats("a", 0)
            for i in range(GT):
                normalize("a", 0, i)
            for i in range(GT):
                combine(0, GT + i)
                tile_stats("a", 1, i)
            group_stats("a", 1)
            for g in range(G):
                attention(g)
            for i in range(GT):
                normalize("f1", G - 1, i)
            route_choose(1)
            route_slots(1)
            route_index(1)
            experts(1)
            for t in range(NT):
                combine(1, t)


def kernel(**inputs):
    import numpy as np
    import concourse.bacc as bacc
    from concourse.bass_utils import run_bass_kernel_spmd

    a = {k.removeprefix("L0_"): np.asarray(v, dtype=None) for k, v in inputs.items()}
    f32 = np.float32
    keep = np.zeros((P, NKEEP), f32)
    p = np.arange(P)
    keep[:, C_ID:C_ID + P] = np.eye(P, dtype=f32)
    keep[:, C_R:C_R + P] = np.arange(P)
    keep[:, C_B:C_B + NBP] = np.arange(NBP)
    keep[:, C_REV16:C_REV16 + 16] = 16 - np.arange(16)
    keep[:, C_REV4:C_REV4 + 4] = 4 - np.arange(4)
    keep[:, C_THR:C_THR + 16] = P * np.arange(16)
    keep[:, C_TK:C_TK + 32] = 1 + np.arange(32)
    keep[:, C_P] = p
    keep[:, C_EMOD] = np.where(p < 3 * E, p % E, -1)
    part = np.full(P, -1)
    part[:3 * E] = np.arange(3 * E) // E
    part[3 * E:3 * E + 6] = np.arange(6) % 3
    for n in range(3):
        keep[:, C_MASK + n] = part == n
    keep[:, C_SB1:C_SB1 + 2] = a["ffn_sb1"].reshape(SF, P).T
    keep[:, C_SB2:C_SB2 + 2] = a["ffn_sb2"].reshape(SF, P).T
    keep[:, C_BQKV:C_BQKV + 3] = a["attn_bqkv"].reshape(3, HD).T
    keep[:, C_RB:C_RB + E] = a["ffn_router_b"]
    keep[:, C_RBIAS:C_RBIAS + E] = a["ffn_router_bias"]
    once = np.zeros((P, NONCE), f32)
    once[:, S_TRI:S_TRI + P] = p[:, None] < p[None, :]
    once[3 * E:3 * E + 3, S_SELS:S_SELS + P] = 1
    once[3 * E + 3:3 * E + 6, S_SELV:S_SELV + P] = 1
    for n in range(3):
        once[n * E:(n + 1) * E, S_B12:S_B12 + FI] = a["ffn_eb1"]
        once[n * E:(n + 1) * E, S_B12 + FI:S_B12 + 2 * FI] = a["ffn_eb2"]
        once[n * E:(n + 1) * E, S_B3:S_B3 + D] = a["ffn_eb3"]
    once[3 * E:3 * E + 3, S_B3:S_B3 + D] = a["ffn_sb3"]
    once[3 * E + 3:3 * E + 6, S_B12:S_B12 + HD] = a["attn_bqkv"][2 * HD:]

    chunks = lambda w: w.reshape(-1, P, w.shape[-1]).transpose(1, 0, 2)
    both = np.stack([a["ffn_ew1"], a["ffn_ew2"]], axis=2)
    arrays = {
        "x_in": a["attn_x"].reshape(T, D),
        "keep_in": keep,
        "once_in": once,
        "rw_in": chunks(a["ffn_router_w"]),
        "w12_in": both.reshape(E, KC, P, 2 * FI).transpose(2, 1, 0, 3).reshape(P, KC, E * 2 * FI),
        "w3_in": a["ffn_ew3"].transpose(1, 0, 2).reshape(P, E * D),
        "sw12_in": chunks(np.concatenate([a["ffn_sw1"], a["ffn_sw2"]], axis=1)),
        "sw3_in": chunks(a["ffn_sw3"]),
        "wqkv_in": chunks(a["attn_Wqkv"]),
        "wo_in": a["attn_Wo"],
        "bo_in": np.broadcast_to(a["attn_bo"], (P, D)),
    }
    arrays = {k: np.ascontiguousarray(v) for k, v in arrays.items()}
    nc = bacc.Bacc("TRN2", target_bir_lowering=False, num_devices=1)
    ins = [nc.dram_tensor(k, v.shape, mybir.dt.from_np(v.dtype), kind="ExternalInput").ap() for k, v in arrays.items()]
    out = nc.dram_tensor("out", (T, D), mybir.dt.float32, kind="ExternalOutput").ap()
    macaron_kernel(nc, *ins, out)
    r = run_bass_kernel_spmd(nc, [arrays], core_ids=[0])
    return r.results[0]["out"].reshape(G, GW, D)
```

```python
import concourse.bass as bass
from concourse import mybir
from contextlib import ExitStack

P = 128
D = 512
KC = D // P
T = 2048
NT = T // P
G = 4
GT = NT // G
GW = GT * P
E = 16
EG = 4
TOPK = 2
FI = 128
SI = 256
SF = SI // P
HD = 128
EPS = 1e-5
SCALE = float(HD) ** -0.5
NB = (TOPK * T + E * (P - 1)) // P
NBP = NB + 1
RING = 4
WS = 32.0
LOW = -3.0e38
OUTSIDE = 1 << 20

C_ID, C_B = 0, 128
C_REV16 = C_B + NBP
C_REV4 = C_REV16 + 16
C_THR = C_REV4 + 4
C_TK = C_THR + 16
C_P = C_TK + 32
C_EMOD = C_P + 1
C_MASK = C_EMOD + 1
C_MASK3 = C_MASK + 3
C_SB1 = C_MASK3 + 3
C_SB2 = C_SB1 + 2
C_BQKV = C_SB2 + 2
C_RB = C_BQKV + 3
C_RBIAS = C_RB + 16
NKEEP = C_RBIAS + 16
S_TRI, S_SELS, S_SELV, S_B12, S_B3 = 0, 128, 256, 384, 640
S_R = S_B3 + D
NONCE = S_R + P


def macaron_kernel(nc, x_in, keep_in, once_in, rw_in, w12_in, w3_in, sw12_in, sw3_in, wqkv_in, wo_in, bo_in, out):
    F32, F16, BF16, I32, U32 = mybir.dt.float32, mybir.dt.float16, mybir.dt.bfloat16, mybir.dt.int32, mybir.dt.uint32
    ALU, ACT, AX = mybir.AluOpType, mybir.ActivationFunctionType, mybir.AxisListType

    with ExitStack() as ctx:
        def sb(name, shape, dt=F32):
            return ctx.enter_context(nc.sbuf_tensor(name, shape, dt))

        def sem(name):
            return ctx.enter_context(nc.semaphore(name))

        bank = [ctx.enter_context(nc.psum_tensor(f"bank{i}", [P, 512], F32)) for i in range(8)]

        w12 = sb("w12", [P, KC * E * 2 * FI])
        w3 = sb("w3", [P, E * D])
        sw12 = sb("sw12", [P, KC, 2, 2 * SI], F16)
        sw3 = sb("sw3", [P, SF, 2, D], F16)
        rw = sb("rw", [P, KC, 2, E], F16)
        keep = sb("keep", [P, NKEEP])
        cnt16 = sb("cnt16", [P, P + TOPK * NT], BF16)
        bo = sb("bo", [P, D])
        x = sb("x", [P, NT, D])
        b12 = sb("b12", [P, 2 * FI], BF16)
        b3 = sb("b3", [P, D], BF16)
        tri = sb("tri", [P, P], BF16)
        ones = sb("ones", [P, P], BF16)
        sel_sb3 = sb("sel_sb3", [P, P], BF16)
        sel_bv = sb("sel_bv", [P, P], BF16)
        eoh = sb("eoh", [P, NBP], BF16)
        gates = sb("gates", [P, TOPK, NT])
        EIDS = 3
        eid = sb("eid", [1, NBP + 4], I32)
        gidx = sb("gidx", [P, NBP], U32)
        sidx = sb("sidx", [P, NBP], U32)
        gi = sb("gi", [P, RING], U32)
        si = sb("si", [P, RING], U32)
        st6 = sb("st6", [P, 2, GT, 6])
        mv = sb("mv", [P, 3 * G, GT, 2])
        veps = sb("veps", [P, 3 * G, GT])
        rstd = sb("rstd", [P, 3 * G, GT])
        mhalf = sb("mhalf", [P, GT])
        nmax = sb("nmax", [P, GT])
        rsum = sb("rsum", [P, GT])
        rinv = sb("rinv", [P, GT])
        s16 = sb("s16", [P, 16 * 6])
        xn = sb("xn", [P, 2, D])
        xT = sb("xT", [P, 3, KC, GW])
        shared = sb("shared", [P, 4 * 512])
        work = sb("work", [P, 5888])

        sh_h = shared[:, 0:1024].rearrange("p (f n) -> p f n", f=SF)
        sh_p = [shared[:, 1536:2048].bitcast(F16).rearrange("p (v n) -> p v n", v=2),
                shared[:, 0:512].bitcast(F16).rearrange("p (v n) -> p v n", v=2)]
        xTp = xT[:, :, :, :].rearrange("p s c n -> p (s c n)").bitcast(F16).rearrange("p (s c v n) -> p s c v n", s=3, c=KC, v=2)
        PIECE = 512
        flat = [w12[:, n * PIECE:(n + 1) * PIECE] for n in range(KC * E * 2 * FI // PIECE)]
        flat += [w3[:, n * PIECE:(n + 1) * PIECE] for n in range(E * D // PIECE)]
        NP = len(flat)
        PIECES = [[0, 0, 4, 0, 2, 2, 2, 2], [2, 2, 2, 2, 2, 2, 2, 2], [2, 2, 2, 2, 1, 1, 1, 1], [0, 0, 0, 0, 2, 2, 2, 2]]
        CUTS = [0, 12, 28, 40, NP]
        LOAD, BEHIND = 4, [4, 5, 6, 7, 8, 10, 12, 14]
        raw_at = flat[2:] + [xn[:, n, :] for n in range(2)]
        w12p = w12[:, :].bitcast(F16).rearrange("p (c m) -> p c m", c=KC)
        w3p = w3[:, :].bitcast(F16)
        raw_sw12 = w3[:, 4096:4096 + KC * 2 * SI].rearrange("p (c n) -> p c n", c=KC)
        raw_sw3 = w3[:, 6144:6144 + SF * D].rearrange("p (f n) -> p f n", f=SF)
        raw_rw = w3[:, 7168:7168 + KC * E].rearrange("p (c n) -> p c n", c=KC)
        sh_u = shared[:, 1024:1536]
        wqkv = work[:, 0:1536].rearrange("p (c n) -> p c n", c=KC)
        wo = work[:, 1536:2048]
        qT, kT = work[:, 2048:2560], work[:, 2560:3072]
        v = work[:, 3072:3584].rearrange("p (t n) -> p t n", t=GT)
        prob = work[:, 3584:4608].rearrange("p (s n) -> p s n", s=2)
        pT = work[:, 4608:5632].rearrange("p (s t n) -> p s t n", s=2, t=GT)
        oT = work[:, 5632:5888].rearrange("p (s n) -> p s n", s=2)
        r32 = [work[:, 5632 + n * TOPK * NT:5632 + (n + 1) * TOPK * NT] for n in range(6)]
        slot_f = r32[0]
        r_h, b_h = (a.bitcast(BF16)[:, 0:TOPK * NT] for a in r32[1:3])
        slot_i, r_i, b_i = (a.bitcast(I32) for a in r32[3:6])
        sh_z = work[:, 4608:5632].rearrange("p (s n) -> p s n", s=2)
        ex1 = xT[:, 1, :, :].rearrange("p c n -> p (c n)")
        ex2 = xT[:, 2, :, :].rearrange("p c n -> p (c n)")
        xg = work[:, 2048:4096].rearrange("p (s n) -> p s n", s=RING)
        xgT = ex1[:, 0:1024].bitcast(F16).rearrange("p (s c v n) -> p s c v n", s=2, c=KC, v=2)
        yo = ex2[:, :].rearrange("p (s n) -> p s n", s=RING)
        e_silu = ex1[:, 1024:1280].rearrange("p (s n) -> p s n", s=2)
        e_h = ex1[:, 1280:1536].rearrange("p (s n) -> p s n", s=2)
        e_hT = ex1[:, 1536:1792].bitcast(F16).rearrange("p (s v n) -> p s v n", s=2, v=2)

        xn_slots = [xn[:, n, :] for n in range(2)] + [work[:, 2048 + n * D:2048 + (n + 1) * D] for n in range(5)]

        ident = keep[:, C_ID:C_ID + P]

        xn_d = [nc.dram_tensor(f"xn_d{l}", [T, D], F32) for l in range(2)]
        y_d = [nc.dram_tensor(f"y_d{l}", [TOPK * T, D], F32) for l in range(2)]

        keep_in_s, once_s, rw_s, x_s = sem("keep_loaded"), sem("once_loaded"), sem("rw_loaded"), [sem(f"x_loaded{g}") for g in range(G)]
        sw12_s, sw3_s, w12_s, w3_s = sem("sw12_loaded"), sem("sw3_loaded"), [sem(f"w12_loaded{n}") for n in range(8)], sem("w3_loaded")
        attw_s, bo_in_s = sem("attn_weights_loaded"), sem("attn_bias_loaded")
        bo_s = sem("attn_bias_added")
        consts_s = sem("consts_ready")
        sb2_s = sem("shared_bias_scaled")
        bn_s = sem("tile_stats_ready")
        mhalf_s, warm_s = sem("mhalf_ready"), sem("first_function_done")
        vstep = sem("vector_step")
        pstep = sem("pool_step")
        var_s = sem("variance_ready")
        rstd_s = sem("rstd_ready")
        xn_s = sem("xn_ready")
        xn_out = [sem(f"xn_stored{n}") for n in range(7)]
        tr_s = sem("transposed")
        trc_s = sem("transposed_copied")
        logit_s = sem("logits_done")
        gu_s = sem("shared_gate_up_done")
        shact_s = sem("shared_act_done")
        shmul_s = sem("shared_mul_done")
        shhi_s, shlo_s = sem("shared_high_parts"), sem("shared_low_parts")
        trlo_s = sem("transposed_low_parts")
        whi_s, wlo_s = sem("weights_high_parts"), sem("weights_low_parts")
        glo_s, ehhi_s = sem("block_low_parts"), sem("block_h_high_parts")
        z_s = sem("shared_out_done")
        zc_s = sem("shared_out_copied")
        zadd_s = sem("shared_added")
        lb_s = sem("router_exp_in")
        ex_s = sem("router_exp_done")
        chosen_s = sem("chosen_ready")
        prefix_s = sem("prefix_done")
        onehot_s = sem("onehots_ready")
        table_s = sem("table_done")
        index_s = sem("indices_ready")
        gi_s, si_s = sem("gather_index"), sem("scatter_index")
        started_s = sem("indirect_dmas_started")
        got_s = [sem(f"gathered{s}") for s in range(RING)]
        put_s = [sem(f"scattered{s}") for s in range(RING)]
        gT_s, gTc_s = sem("block_transposed"), sem("block_transposed_copied")
        egu_s, esilu_s, eh_s = sem("block_gate_up"), sem("block_silu"), sem("block_h")
        ehT_s, ehTc_s = sem("block_h_transposed"), sem("block_h_transposed_copied")
        ed_s, yo_s = sem("block_down"), sem("block_out_ready")
        comb_s = sem("combined")
        qkv_s, qkvc_s = sem("qkv_done"), sem("qkv_copied")
        sc_s, nmax_s, exp_s = sem("scores_done"), sem("row_max_ready"), sem("exp_done")
        pv_s, pvc_s, o_s, att_s = sem("pv_done"), sem("pv_copied"), sem("attn_out_done"), sem("attn_added")
        out_s = sem("out_stored")

        LN_ORDER = [("f0", 0), ("f0", 1), ("f0", 2), ("f0", 3), ("a", 0), ("a", 1), ("f1", 0), ("a", 2), ("f1", 1),
                    ("a", 3), ("f1", 2), ("f1", 3)]
        STAT_ORDER = [("f0", g) for g in range(G)] + [("a", 0), ("a", 1), ("a", 2), ("f1", 0), ("a", 3), ("f1", 1), ("f1", 2), ("f1", 3)]
        LN_AT = {(*key, i): GT * n + i for n, key in enumerate(LN_ORDER) for i in range(GT)}

        def before_scores(g):
            return ("f1", g - 1) if 1 <= g < G - 1 else None

        def beside_softmax(g):
            return ("a", g + 1) if g < G - 1 else ("f1", G - 2)

        fills = [("f0", g, i) for g in range(G) for i in range(GT)] + [("a", 0, i) for i in range(GT)]
        for g in range(G):
            if before_scores(g):
                fills += [(*before_scores(g), i) for i in range(GT)]
            for i in range(GT):
                fills += [("p", g, i), (*beside_softmax(g), i)]
        fills += [("f1", G - 1, i) for i in range(GT)]
        TR_AT = {key: n for n, key in enumerate(fills)}
        lows = lambda n: sum(key[0] in ("f0", "f1") for key in fills[:n + 1])
        LN_TILE = {n: key for key, n in LN_AT.items()}

        XN_AT = [j % len(xn_slots) if j < NT else j % 2 for j in range(GT * len(LN_ORDER))]

        def slot_before(j):
            return [n for n in range(j) if XN_AT[n] == XN_AT[j]]

        def stores_from(slot, tiles):
            return sum(XN_AT[n] == slot and LN_TILE[n][0] != "a" for n in tiles)

        XT_SLOT = {("f0", g): g % 3 for g in range(G)} | {("a", g): 2 for g in range(G)} | {("f1", g): g % 3 for g in range(G)}
        SPLITS = [(raw_rw, rw[:, :, 0, :], rw[:, :, 1, :])]
        SPLITS += [(raw_sw12[:, c, :], sw12[:, c, 0, :], sw12[:, c, 1, :]) for c in range(KC)]
        SPLITS += [(raw_sw3[:, f, :], sw3[:, f, 0, :], sw3[:, f, 1, :]) for f in range(SF)]
        SMALL = len(SPLITS)
        for n in range(NP):
            width = 2 * FI if n < KC * E * 2 * FI // PIECE else D
            parts = flat[n].bitcast(F16).rearrange("p (e v n) -> p e v n", v=2, n=width)
            SPLITS += [(raw_at[n].rearrange("p (e n) -> p e n", n=width), parts[:, :, 0, :], parts[:, :, 1, :])]

        def weights_ready(eng, n):
            if n == 0:
                eng.wait_ge(rw_s, 16)
            elif n == 1:
                eng.wait_ge(sw12_s, 16)
            elif n == 1 + KC:
                eng.wait_ge(sw3_s, 16)
            elif n >= SMALL and n < SMALL + KC * E * 2 * FI // PIECE - 2:
                if (n - SMALL) % LOAD == 0:
                    eng.wait_ge(w12_s[(n - SMALL) // LOAD], 16)
            elif n == SMALL + KC * E * 2 * FI // PIECE - 2:
                eng.wait_ge(w3_s, 48)

        share = lambda tiles, m: list(tiles)[m * len(tiles) // (2 * SF):(m + 1) * len(tiles) // (2 * SF)]
        SH = lambda l, g: l * G + g
        ring_base = lambda l, s: 16 * l * ((NB - s + RING - 1) // RING)
        ring_count = lambda l, b, s: b * (16 // RING) + (ring_base(l, s) - s * (16 // RING))

        places = [shared[:, n * 1024:(n + 1) * 1024] for n in range(2)] + [work[:, 3584 + n * 1024:4608 + n * 1024] for n in range(2)]
        places += [xT[:, n, :, :].rearrange("p c n -> p (c n)")[:, h * 1024:(h + 1) * 1024] for n in range(3) for h in range(2)]
        places += [work[:, n * 1024:(n + 1) * 1024] for n in range(3)]
        yin = [a.rearrange("p (k n) -> p k n", k=TOPK) for a in places]
        YIN_AT = [0, 1, 2, 3, 6, 7, 4, 5] + [0, 1, 6, 7] * 2 + [t % len(yin) for t in range(NT)]
        yin_s = [sem(f"results_loaded{n}") for n in range(len(yin))]
        yin_count = lambda n: 16 * YIN_AT[:n + 1].count(YIN_AT[n])

        block = ctx.enter_context(nc.Block())

        @block.sync
        def _(sp):
            def load_results(l, t):
                n = l * NT + t
                if t == 0:
                    for s in range(RING):
                        sp.wait_ge(put_s[s], ring_base(l + 1, s))
                    sp.wait_ge(zadd_s, NT * (l + 1))
                before = [m for m in range(n) if YIN_AT[m] == YIN_AT[n]]
                if before:
                    sp.wait_ge(comb_s, before[-1] + 1)
                yv = y_d[l].rearrange("(k t p) n -> t p k n", k=TOPK, p=P)
                sp.dma_start(yin[YIN_AT[n]], yv[t]).then_inc(yin_s[YIN_AT[n]], 16)

            xv = x_in.rearrange("(t p) n -> p t n", p=P)
            sp.dma_start(x[:, 0:GT, :], xv[:, 0:GT, :]).then_inc(x_s[0], 16)
            sp.dma_start(raw_rw, rw_in).then_inc(rw_s, 16)
            sp.dma_start(raw_sw12, sw12_in).then_inc(sw12_s, 16)
            sp.dma_start(work[:, 0:NONCE], once_in).then_inc(once_s, 16)
            sp.dma_start(x[:, GT:2 * GT, :], xv[:, GT:2 * GT, :]).then_inc(x_s[1], 16)
            sp.dma_start(raw_sw3, sw3_in).then_inc(sw3_s, 16)
            sp.dma_start(bo[:, :], bo_in).then_inc(bo_in_s, 16)
            for g in range(2, G):
                sp.dma_start(x[:, g * GT:(g + 1) * GT, :], xv[:, g * GT:(g + 1) * GT, :]).then_inc(x_s[g], 16)
            n12 = KC * E * 2 * FI
            for n, tiles in enumerate(BEHIND):
                first, end = n * LOAD * PIECE, min((n + 1) * LOAD * PIECE, n12 - 2 * PIECE)
                sp.wait_ge(trc_s, tiles)
                sp.dma_start(w12[:, 2 * PIECE + first:2 * PIECE + end], w12_in[:, first:end]).then_inc(w12_s[n], 16)
            sp.wait_ge(trc_s, NT)
            sp.wait_ge(wlo_s, SMALL)
            sp.dma_start(w3[:, 0:2 * PIECE], w12_in[:, n12 - 2 * PIECE:]).then_inc(w3_s, 16)
            sp.dma_start(w3[:, 2 * PIECE:], w3_in[:, 0:E * D - 2 * PIECE]).then_inc(w3_s, 16)
            for slot in range(2):
                sp.wait_ge(xn_out[slot], 16 * stores_from(slot, range(NT)))
            sp.dma_start(xn[:, :, :].rearrange("p s n -> p (s n)"), w3_in[:, E * D - 2 * PIECE:]).then_inc(w3_s, 16)
            sp.wait_ge(index_s, 1)
            sp.dma_start(wqkv, wqkv_in).then_inc(attw_s, 16)
            sp.dma_start(wo, wo_in).then_inc(attw_s, 16)
            for l in range(2):
                for t in range(NT):
                    load_results(l, t)

        @block.gpsimd
        def _(pool):
            def rsqrt(n):
                pool.wait_ge(var_s, n + 1)
                pool.tensor_tensor(rstd[:, n, :], veps[:, n, :], mhalf[:, :], ALU.pow).then_inc(rstd_s, 1)

            def shared_part(l, g):
                u = SH(l, g)
                for f in range(SF):
                    pool.wait_ge(shact_s, u * 2 * SF + 2 * f + 2)
                    pool.tensor_tensor(sh_h[:, f, :], sh_h[:, f, :], sh_u, ALU.mult).then_inc(shmul_s, 1)
                    pool.wait_ge(shhi_s, u * SF + f + 1)
                    pool.tensor_tensor(sh_p[f][:, 1, :], sh_h[:, f, :], sh_p[f][:, 0, :], ALU.subtract).then_inc(shlo_s, 1)
                early = g == G - 1
                if early:
                    rows_ready(l)
                for i in range(GT):
                    t = g * GT + i
                    if early:
                        gather(l, i, i)
                    pool.wait_ge(zc_s, u * GT + i + 1)
                    pool.tensor_tensor(x[:, t, :], x[:, t, :], sh_z[:, i % 2, :], ALU.add).then_inc(zadd_s, 1)

            last_token, last_result = pool.to_reg(T - 1), pool.to_reg(TOPK * T - 1)

            def gather(l, b, s):
                pool.tensor_copy(gi[:, s:s + 1], gidx[:, bass.ds(b, 1)]).then_inc(gi_s, 1)
                pool.wait_ge(gi_s, b + (l * NB + 1))
                pool.sem_inc(started_s)
                pool.indirect_dma_start(xg[:, s, :], None, xn_d[l][:, :], bass.IndirectOffsetOnAxis(ap=gi[:, s:s + 1], axis=0),
                                        bounds_check=last_token, oob_is_err=False).then_inc(got_s[s], 16)

            def scatter(l, b, s):
                pool.wait_ge(yo_s, l * NB + b + 1)
                pool.tensor_copy(si[:, s:s + 1], sidx[:, bass.ds(b, 1)]).then_inc(si_s, 1)
                pool.wait_ge(si_s, b + (l * NB + 1))
                pool.sem_inc(started_s)
                pool.indirect_dma_start(y_d[l][:, :], bass.IndirectOffsetOnAxis(ap=si[:, s:s + 1], axis=0), yo[:, s, :], None,
                                        bounds_check=last_result, oob_is_err=False).then_inc(put_s[s], 16)

            def rows_ready(l):
                pool.wait_ge(index_s, l + 1)
                for s in range(len(xn_slots)):
                    pool.wait_ge(xn_out[s], 16 * stores_from(s, range(NT) if l == 0 else range(len(XN_AT))))

            def experts(l):
                whole = (NB - RING) // RING * RING
                with pool.Fori(0, whole, RING) as b:
                    for s in range(RING):
                        pool.wait_ge(gT_s, b + (l * NB + s + 1))
                        gather(l, b + (s + RING), s)
                        scatter(l, b + s, s)
                for b in range(whole, NB):
                    if b + RING < NB:
                        pool.wait_ge(gT_s, l * NB + b + 1)
                        gather(l, b + RING, b % RING)
                    scatter(l, b, b % RING)

            def attn_bias(g):
                for i in range(GT):
                    t = g * GT + i
                    pool.wait_ge(xn_s, LN_AT["a", g, i] + 1)
                    pool.tensor_tensor(x[:, t, :], x[:, t, :], bo[:, :], ALU.add).then_inc(bo_s, 1)

            steps = [0]

            def settle(ins):
                steps[0] += 1
                ins.then_inc(pstep, 1)
                pool.wait_ge(pstep, steps[0])

            pool.memset(mhalf[:, :], -0.5).then_inc(mhalf_s, 1)
            pool.wait_ge(mhalf_s, 1)
            rsqrt(0)
            rsqrt(1)
            pool.wait_ge(once_s, 16)
            pool.wait_ge(keep_in_s, 16)
            raw, acc = work[:, S_B3:S_B3 + D], work[:, 1280:1280 + D]
            hi, mid = work[:, 1792:2048].bitcast(BF16), work[:, 4608:4864].bitcast(BF16)
            pool.tensor_copy(sel_sb3[:, :], work[:, S_SELS:S_SELS + P])
            settle(pool.tensor_copy(hi, raw))
            settle(pool.tensor_tensor(raw, raw, hi, ALU.subtract))
            settle(pool.tensor_copy(mid, raw))
            settle(pool.tensor_tensor(raw, raw, mid, ALU.subtract))
            rsqrt(2)
            mask = lambda k: keep[:, C_MASK3 + k:C_MASK3 + k + 1].to_broadcast([P, D])
            pool.tensor_tensor(acc, hi, mask(0), ALU.mult)
            settle(pool.tensor_tensor(raw, raw, mask(2), ALU.mult))
            settle(pool.tensor_tensor(acc, acc, raw, ALU.add))
            settle(pool.tensor_tensor(raw, mid, mask(1), ALU.mult))
            settle(pool.tensor_tensor(acc, acc, raw, ALU.add))
            pool.tensor_copy(b3[:, :], acc).then_inc(consts_s, 1)
            rsqrt(3)
            for g in range(G):
                shared_part(0, g)
            experts(0)
            pool.wait_ge(bo_in_s, 16)
            rsqrt(STAT_ORDER.index(("a", 0)))
            rsqrt(STAT_ORDER.index(("a", 1)))
            for g in range(G):
                attn_bias(g)
                if g + 2 < G:
                    rsqrt(STAT_ORDER.index(("a", g + 2)))
                rsqrt(STAT_ORDER.index(("f1", g)))
            for g in range(G):
                shared_part(1, g)
            experts(1)

        @block.scalar
        def _(act):
            def copy_T(kind, g, i):
                k = TR_AT[kind, g, i]
                act.wait_ge(tr_s, k + 1)
                if kind == "p":
                    dst = pT[:, i % 2, :, :]
                else:
                    dst = xT[:, XT_SLOT[kind, g], :, i * P:(i + 1) * P]
                if kind in ("f0", "f1"):
                    dst = xTp[:, XT_SLOT[kind, g], :, 0, i * P:(i + 1) * P]
                if kind in ("f0", "f1"):
                    t = g * GT + i
                    slot = XN_AT[LN_AT[kind, g, i]]
                    act.dma_start(xn_d[int(kind[1])][t * P:(t + 1) * P, :], xn_slots[slot]).then_inc(xn_out[slot], 16)
                nc.scalar.activation(dst, bank[k % 2][:, :].rearrange("p (c n) -> p c n", c=KC), ACT.Copy).then_inc(trc_s, 1)

            def shared_part(l, g, beside_gate_up=(), beside_down=()):
                u = SH(l, g)

                def spread(q):
                    if l == 0:
                        high_parts(SMALL + sum(map(sum, PIECES[:g])) + sum(PIECES[g][:q]), PIECES[g][q])

                beside_down = list(beside_down)
                def high_part(f):
                    act.wait_ge(shmul_s, u * SF + f + 1)
                    nc.scalar.activation(sh_p[f][:, 0, :], sh_h[:, f, :], ACT.Copy).then_inc(shhi_s, 1)

                for m in range(2 * SF):
                    act.wait_ge(gu_s, u * 2 * SF + m + 1)
                    f = m // 2
                    if m % 2 == 0:
                        if u:
                            act.wait_ge(z_s, u * GT)
                        nc.scalar.activation(sh_h[:, f, :], bank[3][:, :], ACT.Silu, bias=keep[:, C_SB1 + f:C_SB1 + f + 1],
                                             scale=1.0 / WS).then_inc(shact_s, 1)
                    else:
                        if u or f:
                            act.wait_ge(shmul_s, u * SF + f)
                        nc.scalar.activation(sh_u, bank[4][:, :], ACT.Identity, bias=keep[:, C_SB2 + f:C_SB2 + f + 1]).then_inc(shact_s, 1)
                    for tile in share(beside_gate_up, m):
                        copy_T(*tile)
                    if m == 2:
                        high_part(0)
                    if m < 2 * SF - 1:
                        spread(m)
                high_part(1)
                spread(2 * SF - 1)
                for i in range(GT):
                    n = u * GT + i
                    act.wait_ge(z_s, n + 1)
                    if n >= 2:
                        act.wait_ge(zadd_s, n - 1)
                    nc.scalar.activation(sh_z[:, i % 2, :], bank[5 + n % 3][:, :], ACT.Copy, scale=0.5 / (WS * WS)).then_inc(zc_s, 1)
                    if beside_down:
                        copy_T(*beside_down.pop(0))
                    spread(2 * SF + i)

            def attn_copies(g, n):
                act.wait_ge(qkv_s, 3 * g + n + 1)
                if n < 2:
                    nc.scalar.activation([qT, kT][n], bank[3 + n][:, :], ACT.Identity, bias=keep[:, C_BQKV + n:C_BQKV + n + 1]).then_inc(qkvc_s, 1)
                else:
                    nc.scalar.activation(v, bank[5][:, :].rearrange("p (t n) -> p t n", t=GT), ACT.Copy).then_inc(qkvc_s, 1)

            def exp(g, i):
                act.wait_ge(nmax_s, g * GT + i + 1)
                nc.scalar.activation(prob[:, i % 2, :], bank[3 + i % 2][:, :], ACT.Exp, bias=nmax[:, i:i + 1], scale=SCALE,
                                     accum_out=rsum[:, i:i + 1]).then_inc(exp_s, 1)

            def copy_pv(g, i):
                n = g * GT + i
                act.wait_ge(pv_s, n + 1)
                nc.scalar.activation(oT[:, i % 2, :], bank[6][:, 0:P], ACT.Copy).then_inc(pvc_s, 1)

            def attention(g):
                attn_copies(g, 0)
                attn_copies(g, 1)
                if before_scores(g):
                    copy_T(*before_scores(g), 0)
                    copy_T(*before_scores(g), 1)
                exp(g, 0)
                exp(g, 1)
                if before_scores(g):
                    copy_T(*before_scores(g), 2)
                    copy_T(*before_scores(g), 3)
                attn_copies(g, 2)
                copy_T("p", g, 0)
                for i in range(GT):
                    if i < GT - 1:
                        copy_T(*beside_softmax(g), i)
                        copy_T("p", g, i + 1)
                    copy_pv(g, i)
                    if i + 2 < GT:
                        exp(g, i + 2)
                copy_T(*beside_softmax(g), GT - 1)

            def router_exp(l):
                act.wait_ge(lb_s, l + 1)
                nc.scalar.activation(work[:, 0:NT * E], work[:, 0:NT * E], ACT.Exp).then_inc(ex_s, 1)

            def block_act(l, b, s):
                q = l * NB + b
                act.wait_ge(egu_s, q + 1)
                nc.scalar.activation(e_silu[:, s, :], bank[3 + s][:, 0:FI], ACT.Silu, scale=1.0 / WS).then_inc(esilu_s, 1)

            def block_copy_T(l, b, s):
                act.wait_ge(gT_s, b + (l * NB + 1))
                nc.scalar.activation(xgT[:, s, :, 0, :], bank[s][:, :].rearrange("p (c n) -> p c n", c=KC), ACT.Copy).then_inc(gTc_s, 1)

            def experts(l):
                block_copy_T(l, 0, 0)
                with act.Fori(0, NB - 1, 2) as b:
                    for s in range(2):
                        block_act(l, b + s, s)
                        block_copy_T(l, b + (s + 1), 1 - s)
                block_act(l, NB - 1, 0)

            def high_piece(j):
                weights_ready(act, j)
                if j >= SMALL + 2:
                    act.wait_ge(wlo_s, j - 1)
                nc.scalar.activation(SPLITS[j][1], SPLITS[j][0], ACT.Copy, scale=WS).then_inc(whi_s, 1)

            def high_parts(first, n):
                for j in range(first, first + n):
                    high_piece(j)

            act.dma_start(keep[:, :], keep_in).then_inc(keep_in_s, 16)
            act.wait_ge(mhalf_s, 1)
            nc.scalar.activation(nmax[:, :], mhalf[:, :], ACT.Silu).then_inc(warm_s, 1)
            act.wait_ge(keep_in_s, 16)
            for i in range(2):
                copy_T("f0", 0, i)
            high_parts(0, 1)
            for i in range(2, GT):
                copy_T("f0", 0, i)
            high_parts(1, SMALL - 1)
            act.wait_ge(sb2_s, 1)
            shared_part(0, 0, [("f0", g, i) for g in (1, 2) for i in range(GT)], [("f0", 3, i) for i in range(GT)])
            router_exp(0)
            for g in range(1, G):
                shared_part(0, g)
            experts(0)
            for i in range(GT):
                copy_T("a", 0, i)
            for g in range(G):
                attention(g)
            shared_part(1, 0, (), [("f1", 3, i) for i in range(GT)])
            router_exp(1)
            for g in range(1, G):
                shared_part(1, g)
            experts(1)
            for t in range(NT):
                act.wait_ge(comb_s, NT + t + 1)
                act.dma_start(out[t * P:(t + 1) * P, :], x[:, t, :]).then_inc(out_s, 16)
            act.wait_ge(out_s, 16 * NT)

        @block.tensor
        def _(pe):
            def bank_free(k):
                if k >= 2:
                    pe.wait_ge(trc_s, k - 1)
                    if lows(k - 2):
                        pe.wait_ge(trlo_s, lows(k - 2))

            def product(o, lhs, rhs, start, stop):
                for l_part, r_part in ((0, 0), (0, 1), (1, 0)):
                    ins = pe.matmul(o, lhs(l_part), rhs(r_part), start=start and l_part + r_part == 0, stop=stop and l_part == 1)
                return ins

            def fill_T(kind, g, i):
                k = TR_AT[kind, g, i]
                pe.wait_ge(xn_s, LN_AT[kind, g, i] + 1)
                bank_free(k)
                for c in range(KC):
                    ins = pe.transpose(bank[k % 2][:, c * P:(c + 1) * P], xn_slots[XN_AT[LN_AT[kind, g, i]]][:, c * P:(c + 1) * P], ident)
                ins.then_inc(tr_s, 1)

            def router(l, g, i):
                kind = f"f{l}"
                t = g * GT + i
                pe.wait_ge(trlo_s, lows(TR_AT[kind, g, i]))
                if t == 0 and l == 0:
                    pe.wait_ge(wlo_s, 1)
                o = bank[2][:, t * 2 * E:(t + 1) * 2 * E]
                tokens = xTp[:, XT_SLOT[kind, g], :, :, i * P:(i + 1) * P]
                both = lambda c: pe.matmul(o, tokens[:, c, 0, :], rw[:, c, :, :].rearrange("p v n -> p (v n)"), start=(c == 0),
                                           stop=(c == KC - 1))
                for c in range(KC - 1):
                    both(c)
                for c in range(KC):
                    pe.matmul(o[:, 0:E], tokens[:, c, 1, :], rw[:, c, 0, :], start=False, stop=False)
                ins = both(KC - 1)
                ins.then_inc(logit_s, 1)

            waiting = []

            def fill(kind, g, i):
                fill_T(kind, g, i)
                flush()
                if kind != "a":
                    waiting.append((int(kind[1]), g, i))

            def flush():
                while waiting:
                    router(*waiting.pop(0))

            def shared_part(l, g, beside_gate_up=(), beside_down=(), between=None):
                u = SH(l, g)
                beside_down = list(beside_down)
                src = xTp[:, XT_SLOT[f"f{l}", g], :, :, :]
                pe.wait_ge(trlo_s, lows(TR_AT[f"f{l}", g, GT - 1]))
                if u == 0:
                    pe.wait_ge(wlo_s, 1 + KC)
                for m in range(2 * SF):
                    if u * 2 * SF + m >= 2:
                        pe.wait_ge(shact_s, u * 2 * SF + m - 1)
                    col = (m // 2) * P + (m % 2) * SI
                    for c in range(KC):
                        ins = product(bank[3 + m % 2][:, :], lambda v: sw12[:, c, v, col:col + P], lambda v: src[:, c, v, :],
                                      c == 0, c == KC - 1)
                    ins.then_inc(gu_s, 1)
                    for tile in share(beside_gate_up, m):
                        fill(*tile)

                if between:
                    between(l)

                def down(i, f):
                    n = u * GT + i
                    o = bank[5 + n % 3][:, :]
                    if f == 0:
                        if n >= 3:
                            pe.wait_ge(zc_s, n - 2)
                        if l and g == 0 and n % 3 == 2:
                            pe.wait_ge(att_s, NT)
                    lhs, rhs = sh_p[f][:, :, i * P:(i + 1) * P], sw3[:, f, :, :]
                    pe.wait_ge(shhi_s, u * SF + f + 1)
                    pe.matmul(o, lhs[:, 0, :], rhs[:, 0, :], start=(f == 0), stop=False)
                    pe.matmul(o, lhs[:, 0, :], rhs[:, 1, :], start=False, stop=False)
                    pe.wait_ge(shlo_s, u * SF + f + 1)
                    pe.matmul(o, lhs[:, 1, :], rhs[:, 0, :], start=False, stop=False)
                    if f == SF - 1:
                        if n == 0:
                            pe.wait_ge(consts_s, 1)
                        pe.matmul(o, sel_sb3[:, :], b3[:, :], start=False, stop=True).then_inc(z_s, 1)
                        if beside_down:
                            fill(*beside_down.pop(0))

                if u == 0:
                    pe.wait_ge(wlo_s, SMALL)
                for i, f in ((0, 0), (1, 0), (2, 0), (0, 1), (1, 1), (2, 1), (3, 0), (3, 1)):
                    down(i, f)
                flush()

            def prefix(l):
                chosen = work[:, 4480:4608].bitcast(BF16)
                pe.wait_ge(chosen_s, l + 1)
                pe.wait_ge(trlo_s, NT * (l + 1))
                pe.matmul(bank[0][:, 0:NT * E], tri[:, :], chosen, start=True, stop=True)
                pe.matmul(bank[1][:, 0:NT * E], ones[:, :], chosen, start=True, stop=True).then_inc(prefix_s, 1)

            def table(l):
                ohr = work[:, 0:2048].bitcast(BF16)
                obv = work[:, 2048:2048 + 48 * 32].bitcast(BF16)
                pe.wait_ge(onehot_s, l + 1)
                for n in range(TOPK * NT):
                    ins = pe.matmul(bank[0][:, 0:2 * NBP], ohr[:, n * P:(n + 1) * P], obv[:, n * 2 * NBP:(n + 1) * 2 * NBP],
                                    start=(n == 0), stop=(n == TOPK * NT - 1))
                ins.then_inc(table_s, 1)

            def qkv(g, n):
                src = xT[:, XT_SLOT["a", g], :, :]
                if n == 0:
                    pe.wait_ge(trc_s, TR_AT["a", g, GT - 1] + 1)
                    if g:
                        pe.wait_ge(exp_s, g * GT)
                if n < 2:
                    for c in range(KC):
                        ins = pe.matmul(bank[3 + n][:, :], wqkv[:, c, n * HD:(n + 1) * HD], src[:, c, :], start=(c == 0), stop=(c == KC - 1))
                    ins.then_inc(qkv_s, 1)
                    return
                if g:
                    pe.wait_ge(qkvc_s, 3 * g)
                for i in range(GT):
                    for c in range(KC):
                        ins = pe.matmul(bank[5][:, i * P:(i + 1) * P], src[:, c, i * P:(i + 1) * P], wqkv[:, c, 2 * HD:3 * HD],
                                        start=(c == 0), stop=False)
                    ins = pe.matmul(bank[5][:, i * P:(i + 1) * P], sel_bv[:, :], b12[:, 0:HD], start=False, stop=True)
                ins.then_inc(qkv_s, 1)

            def scores(g, i):
                if i == 0:
                    pe.wait_ge(qkvc_s, 3 * g + 2)
                if i >= 2:
                    pe.wait_ge(exp_s, g * GT + i - 1)
                pe.matmul(bank[3 + i % 2][:, :], qT[:, i * P:(i + 1) * P], kT, start=True, stop=True).then_inc(sc_s, 1)

            def probs_T(g, i):
                k = TR_AT["p", g, i]
                pe.wait_ge(exp_s, g * GT + i + 1)
                bank_free(k)
                for t in range(GT):
                    ins = pe.transpose(bank[k % 2][:, t * P:(t + 1) * P], prob[:, i % 2, t * P:(t + 1) * P], ident)
                ins.then_inc(tr_s, 1)

            def pv(g, i):
                n = g * GT + i
                pe.wait_ge(trc_s, TR_AT["p", g, i] + 1)
                pe.wait_ge(qkvc_s, 3 * g + 3)
                if n:
                    pe.wait_ge(pvc_s, n)
                for t in range(GT):
                    ins = pe.matmul(bank[6][:, 0:P], v[:, t, :], pT[:, i % 2, t, :], start=(t == 0), stop=(t == GT - 1))
                ins.then_inc(pv_s, 1)

            def out_proj(g, i):
                n = g * GT + i
                pe.wait_ge(pvc_s, n + 1)
                if n:
                    pe.wait_ge(att_s, n)
                pe.matmul(bank[7][:, :], oT[:, i % 2, :], wo, start=True, stop=True).then_inc(o_s, 1)

            def attention(g):
                qkv(g, 0)
                qkv(g, 1)
                if before_scores(g):
                    for i in range(2):
                        fill_T(*before_scores(g), i)
                        waiting.append((1, before_scores(g)[1], i))
                scores(g, 0)
                scores(g, 1)
                flush()
                if before_scores(g):
                    for i in range(2, GT):
                        fill_T(*before_scores(g), i)
                        waiting.append((1, before_scores(g)[1], i))
                qkv(g, 2)
                flush()
                probs_T(g, 0)
                for i in range(GT):
                    if i + 2 < GT:
                        scores(g, i + 2)
                    if i < GT - 1:
                        fill(*beside_softmax(g), i)
                        probs_T(g, i + 1)
                    pv(g, i)
                    if i:
                        out_proj(g, i - 1)
                fill(*beside_softmax(g), GT - 1)
                out_proj(g, GT - 1)
                flush()

            def block_T(l, b, r):
                s = r % 2
                pe.wait_ge(got_s[r], ring_count(l, b, r) + 16)
                if not (l == 0 and isinstance(b, int) and b < 2):
                    pe.wait_ge(glo_s, b + (l * NB - 1))
                for c in range(KC):
                    ins = pe.transpose(bank[s][:, c * P:(c + 1) * P], xg[:, r, c * P:(c + 1) * P], ident)
                ins.then_inc(gT_s, 1)

            def experts_of(b, n):
                _, ids = nc.values_load_multi_w_load_instructions(eid[0:1, bass.ds(b + EIDS, n)], engines=(mybir.EngineType.PE,),
                                                                  min_val=0, max_val=E - 1,
                                                                  skip_runtime_bounds_check_because="counts from 0 on, held to E - 1 by a minimum")
                return ids

            def block_gate_up(l, b, s, e):
                pe.wait_ge(gTc_s, b + (l * NB + 1))
                if not (l == 0 and isinstance(b, int) and b < 2):
                    pe.wait_ge(eh_s, b + (l * NB - 1))
                o = bank[3 + s][:, 0:2 * FI]
                pe.matmul(o, eoh[:, bass.ds(b, 1)].to_broadcast([P, P]), b12[:, :], start=True, stop=False)
                weights = lambda c, v: w12p[:, c, bass.ds(e * (4 * FI) + v * 2 * FI, 2 * FI)]
                for c in range(KC):
                    pe.matmul(o, xgT[:, s, c, 0, :], weights(c, 0), start=False, stop=False)
                    pe.matmul(o, xgT[:, s, c, 0, :], weights(c, 1), start=False, stop=False)
                pe.wait_ge(glo_s, b + (l * NB + 1))
                for c in range(KC):
                    ins = pe.matmul(o, xgT[:, s, c, 1, :], weights(c, 0), start=False, stop=(c == KC - 1))
                ins.then_inc(egu_s, 1)

            def block_h_T(l, b, s):
                pe.wait_ge(eh_s, b + (l * NB + 1))
                if not (l == 0 and isinstance(b, int) and b == 0):
                    pe.wait_ge(ehTc_s, b + l * NB)
                pe.transpose(bank[5][:, 0:P], e_h[:, s, :], ident).then_inc(ehT_s, 1)

            def block_down(l, b, s, e):
                pe.wait_ge(ehTc_s, b + (l * NB + 1))
                if not (l == 0 and isinstance(b, int) and b < 2):
                    pe.wait_ge(yo_s, b + (l * NB - 1))
                o = bank[6 + s][:, :]
                pe.matmul(o, eoh[:, bass.ds(b, 1)].to_broadcast([P, P]), b3[:, :], start=True, stop=False)
                product(o, lambda v: e_hT[:, s, v, :], lambda v: w3p[:, bass.ds(e * (2 * D) + v * D, D)], False, True).then_inc(ed_s, 1)

            def experts(l):
                pe.wait_ge(index_s, l + 1)
                block_T(l, 0, 0)
                if l == 0:
                    pe.wait_ge(wlo_s, SMALL + NP)
                def step(b, s, r, e, e_before):
                    block_gate_up(l, b, s, e)
                    if not (isinstance(b, int) and b == NB - 1):
                        block_T(l, b + 1, r)
                    if e_before is not None:
                        block_down(l, b - 1, 1 - s, e_before)
                    if isinstance(b, int) and b == 0:
                        pe.wait_ge(zc_s, NT * (l + 1))
                    block_h_T(l, b, s)

                turn = 3 * RING
                first = (NB - 1) % turn
                ids = experts_of(0, first)
                step(0, 0, 1, ids[0], None)
                for b in range(1, first):
                    step(b, b % 2, (b + 1) % RING, ids[b], ids[b - 1])
                with pe.Fori(0, (NB - 1) // turn) as n:
                    b = n * turn + first
                    ids = experts_of(b - 1, turn + 1)
                    for u in range(turn):
                        step(b + u, (first + u) % 2, (first + u + 1) % RING, ids[u + 1], ids[u])
                ids = experts_of(NB - 2, 2)
                step(NB - 1, 0, None, ids[1], ids[0])
                block_down(l, NB - 1, 0, ids[1])

            pe.wait_ge(keep_in_s, 16)
            for i in range(GT):
                fill("f0", 0, i)
            flush()
            shared_part(0, 0, [("f0", g, i) for g in (1, 2) for i in range(GT)], [("f0", 3, i) for i in range(GT)])
            shared_part(0, 1)
            shared_part(0, 2, between=prefix)
            shared_part(0, 3, between=table)
            experts(0)
            for i in range(GT):
                fill("a", 0, i)
            pe.wait_ge(attw_s, 32)
            for g in range(G):
                attention(g)
            shared_part(1, 0, (), [("f1", 3, i) for i in range(GT)])
            shared_part(1, 1)
            prefix(1)
            shared_part(1, 2)
            shared_part(1, 3, between=table)
            experts(1)

        @block.vector
        def _(ve):
            steps = [0]

            beside = []

            def settle(ins):
                steps[0] += 1
                ins.then_inc(vstep, 1)
                if beside and steps[0] % 3:
                    low_parts(beside.pop(0), 1)
                ve.wait_ge(vstep, steps[0])

            def kc(c, n):
                return keep[:, c:c + n]

            def combine(l, t):
                n = l * NT + t
                ve.wait_ge(yin_s[YIN_AT[n]], yin_count(n))
                y = yin[YIN_AT[n]]
                settle(ve.scalar_tensor_tensor(out=x[:, t, :], in0=y[:, 0, :], scalar=gates[:, 0, t:t + 1],
                                               in1=x[:, t, :], op0=ALU.mult, op1=ALU.add))
                ve.scalar_tensor_tensor(out=x[:, t, :], in0=y[:, 1, :], scalar=gates[:, 1, t:t + 1],
                                        in1=x[:, t, :], op0=ALU.mult, op1=ALU.add).then_inc(comb_s, 1)

            def low_part(kind, g, i):
                k = TR_AT[kind, g, i]
                ve.wait_ge(trc_s, k + 1)
                to = xTp[:, XT_SLOT[kind, g], :, :, i * P:(i + 1) * P]
                ve.tensor_tensor(to[:, :, 1, :], bank[k % 2][:, :].rearrange("p (c n) -> p c n", c=KC), to[:, :, 0, :],
                                 ALU.subtract).then_inc(trlo_s, 1)

            def low_parts(first, n):
                for j in range(first, first + n):
                    weights_ready(ve, j)
                    ve.wait_ge(whi_s, j + 1)
                    w, high, low = SPLITS[j]
                    ve.scalar_tensor_tensor(out=low, in0=w, scalar=WS, in1=high, op0=ALU.mult, op1=ALU.subtract).then_inc(wlo_s, 1)

            def tile_stats(kind, g, i):
                if kind == "f0":
                    ve.wait_ge(x_s[g], 16)
                elif kind == "a":
                    ve.wait_ge(comb_s, g * GT + i + 1)
                else:
                    ve.wait_ge(att_s, g * GT + i + 1)
                ve.bn_stats(st6[:, kind == "a", i, :], x[:, g * GT + i, :]).then_inc(bn_s, 1)

            def group_stats(kind, g):
                n = STAT_ORDER.index((kind, g))
                ve.wait_ge(bn_s, (n + 1) * GT)
                for i in range(GT):
                    ins = ve.bn_aggr(mv[:, n, i, :], st6[:, kind == "a", i, :])
                settle(ins)
                ve.tensor_scalar(veps[:, n, :], mv[:, n, :, 1], EPS, None, ALU.add).then_inc(var_s, 1)

            def stats(kind, g):
                for i in range(GT):
                    tile_stats(kind, g, i)
                group_stats(kind, g)

            def normalize(kind, g, i):
                n = STAT_ORDER.index((kind, g))
                j = LN_AT[kind, g, i]
                if i == 0:
                    ve.wait_ge(rstd_s, n + 1)
                if slot_before(j):
                    ve.wait_ge(tr_s, TR_AT[LN_TILE[slot_before(j)[-1]]] + 1)
                    ve.wait_ge(xn_out[XN_AT[j]], 16 * stores_from(XN_AT[j], range(j)))
                ve.tensor_scalar(xn_slots[XN_AT[j]], x[:, g * GT + i, :], mv[:, n, i, 0:1], rstd[:, n, i:i + 1], ALU.subtract,
                                 ALU.mult).then_inc(xn_s, 1)

            def attention(g):
                def row_max(i):
                    if g == 0 and i == 0:
                        ve.wait_ge(warm_s, 1)
                    ve.wait_ge(sc_s, g * GT + i + 1)
                    settle(ve.tensor_reduce(nmax[:, i:i + 1], bank[3 + i % 2][:, :], AX.X, ALU.max))
                    ve.tensor_scalar(nmax[:, i:i + 1], nmax[:, i:i + 1], -SCALE, None, ALU.mult).then_inc(nmax_s, 1)

                def add(i):
                    t = g * GT + i
                    ve.wait_ge(exp_s, t + 1)
                    settle(ve.reciprocal(rinv[:, i:i + 1], rsum[:, i:i + 1]))
                    ve.wait_ge(o_s, t + 1)
                    ve.wait_ge(bo_s, t + 1)
                    ve.scalar_tensor_tensor(out=x[:, t, :], in0=bank[7][:, :], scalar=rinv[:, i:i + 1], in1=x[:, t, :],
                                            op0=ALU.mult, op1=ALU.add).then_inc(att_s, 1)

                def combine_ahead(tiles):
                    if g + 2 < G:
                        for i in tiles:
                            combine(0, (g + 2) * GT + i)
                            tile_stats("a", g + 2, i)

                before, beside = before_scores(g), beside_softmax(g)
                if before:
                    normalize(*before, 0)
                    normalize(*before, 1)
                combine_ahead(range(GT // 2))
                if before:
                    low_part(*before, 0)
                    low_part(*before, 1)
                    normalize(*before, 2)
                    normalize(*before, 3)
                row_max(0)
                row_max(1)
                if before:
                    low_part(*before, 2)
                    low_part(*before, 3)
                normalize(*beside, 0)
                combine_ahead(range(GT // 2, GT))
                if g + 2 < G:
                    group_stats("a", g + 2)
                for i in range(GT):
                    if i + 2 < GT:
                        row_max(i + 2)
                    if i + 1 < GT:
                        normalize(*beside, i + 1)
                    if beside[0] != "a" and i < GT - 1:
                        low_part(*beside, i)
                    if i:
                        add(i - 1)
                        tile_stats("f1", g, i - 1)
                if beside[0] != "a":
                    low_part(*beside, GT - 1)
                add(GT - 1)
                tile_stats("f1", g, GT - 1)
                group_stats("f1", g)

            def first_max(out, vals, tmp, red, rev, shape):
                n = shape[-1]
                settle(ve.tensor_reduce(red, vals, AX.X, ALU.max))
                settle(ve.tensor_tensor(tmp, vals, red.unsqueeze(2).to_broadcast(shape), ALU.is_equal))
                settle(ve.tensor_tensor(tmp, tmp, rev, ALU.mult))
                settle(ve.tensor_reduce(red, tmp, AX.X, ALU.max))
                settle(ve.tensor_tensor(out, tmp, red.unsqueeze(2).to_broadcast(shape), ALU.is_equal))

            NE = NT * E
            A = [work[:, n * NE:(n + 1) * NE] for n in range(8)]
            te = lambda a: a.rearrange("p (t e) -> p t e", e=E)
            S3 = [P, NT, E]

            def route_choose(l, pieces=()):
                lg, tmp, sc, ms = A[0], A[1], A[2], A[3]
                oh = [A[4], A[5]]
                red = s16[:, 0:16]
                gm, gk, gt_, g1 = (A[6][:, 64 * n:64 * n + 64].rearrange("p (t j) -> p t j", j=EG) for n in range(4))
                ve.wait_ge(logit_s, (l + 1) * NT)
                halves = bank[2][:, :].rearrange("p (t v e) -> p t v e", t=NT, v=2)
                settle(ve.scalar_tensor_tensor(out=te(tmp), in0=halves[:, :, 0, :], scalar=1.0 / WS,
                                               in1=kc(C_RB, E).unsqueeze(1).to_broadcast(S3), op0=ALU.mult, op1=ALU.add))
                settle(ve.scalar_tensor_tensor(out=te(lg), in0=halves[:, :, 1, :], scalar=1.0 / WS, in1=te(tmp), op0=ALU.mult,
                                               op1=ALU.add))
                settle(ve.tensor_reduce(red, te(lg), AX.X, ALU.max))
                ve.tensor_tensor(te(lg), te(lg), red.unsqueeze(2).to_broadcast(S3), ALU.subtract).then_inc(lb_s, 1)
                ve.wait_ge(ex_s, l + 1)
                beside.extend(pieces)
                settle(ve.tensor_reduce(red, te(lg), AX.X, ALU.add))
                settle(ve.reciprocal(red, red))
                settle(ve.tensor_tensor(te(sc), te(lg), red.unsqueeze(2).to_broadcast(S3), ALU.mult))
                settle(ve.tensor_tensor(te(sc), te(sc), kc(C_RBIAS, E).unsqueeze(1).to_broadcast(S3), ALU.add))
                sh4 = [P, NT, EG]
                rev4 = kc(C_REV4, EG).unsqueeze(1).to_broadcast(sh4)
                settle(ve.tensor_reduce(gm.rearrange("p t j -> p (t j)"), sc.rearrange("p (a b) -> p a b", b=E // EG), AX.X, ALU.max))
                first_max(g1, gm, gt_, red, rev4, sh4)
                settle(ve.tensor_copy(gk, g1))
                settle(ve.scalar_tensor_tensor(out=gm, in0=g1, scalar=LOW, in1=gm, op0=ALU.mult, op1=ALU.add))
                first_max(g1, gm, gt_, red, rev4, sh4)
                settle(ve.tensor_tensor(gk, gk, g1, ALU.add))
                settle(ve.tensor_scalar(gk, gk, -1.0, -LOW, ALU.add, ALU.mult))
                s64 = [P, NT * EG, E // EG]
                settle(ve.tensor_tensor(ms.rearrange("p (a b) -> p a b", b=E // EG), sc.rearrange("p (a b) -> p a b", b=E // EG),
                                        gk.rearrange("p t j -> p (t j)").unsqueeze(2).to_broadcast(s64), ALU.add))
                rev16 = kc(C_REV16, E).unsqueeze(1).to_broadcast(S3)
                for k in range(TOPK):
                    first_max(te(oh[k]), te(ms), te(tmp), red, rev16, S3)
                    settle(ve.tensor_tensor(tmp, oh[k], sc, ALU.mult))
                    settle(ve.tensor_reduce(red, te(tmp), AX.X, ALU.add))
                    if k == 0:
                        settle(ve.scalar_tensor_tensor(out=ms, in0=oh[0], scalar=LOW, in1=ms, op0=ALU.mult, op1=ALU.add))
                    settle(ve.tensor_scalar(gates[:, k, :], red, 0.5 / (WS * WS), None, ALU.mult))
                chosen = work[:, 4480:4608].bitcast(BF16)
                ve.tensor_tensor(chosen, oh[0], oh[1], ALU.add).then_inc(chosen_s, 1)

            def route_slots(l):
                oh = [A[4], A[5]]
                tot = [work[:, 6 * NE + n * 384:6 * NE + (n + 1) * 384].rearrange("p (t e) -> p t e", e=E) for n in range(2)]
                PAD = 8
                cnt, nblk, start, tmp16, end = (s16[:, 16 * n:16 * n + 16] for n in range(1, 6))
                cmp = A[0].rearrange("p (a b) -> p a b", b=16)
                slot = te(A[1])
                ve.wait_ge(prefix_s, l + 1)
                ve.memset(tot[0][:, 0:PAD, :], 0.0)
                ve.memset(tot[1][:, 0:PAD, :], 0.0)
                settle(ve.tensor_copy(tot[0][:, PAD:, :], te(bank[1][:, 0:NE])))
                for n, d in enumerate((1, 2, 4, 8)):
                    a, b = tot[n % 2], tot[1 - n % 2]
                    settle(ve.tensor_tensor(b[:, PAD:, :], a[:, PAD:, :], a[:, PAD - d:PAD + NT - d, :], ALU.add))
                incl = tot[0]
                settle(ve.tensor_copy(cnt, incl[:, PAD + NT - 1, :]))
                sh = [P, E, 16]
                settle(ve.tensor_tensor(cmp, cnt.unsqueeze(2).to_broadcast(sh), kc(C_THR, 16).unsqueeze(1).to_broadcast(sh), ALU.is_gt))
                settle(ve.tensor_reduce(nblk, cmp, AX.X, ALU.add))
                settle(ve.tensor_tensor(cmp, kc(C_THR, 16).unsqueeze(2).to_broadcast(sh), kc(C_THR, 16).unsqueeze(1).to_broadcast(sh), ALU.is_gt))
                settle(ve.tensor_tensor(cmp, cmp, nblk.unsqueeze(1).to_broadcast(sh), ALU.mult))
                settle(ve.tensor_reduce(start, cmp, AX.X, ALU.add))
                settle(ve.tensor_tensor(end, start, nblk, ALU.add))
                settle(ve.tensor_scalar(start, start, float(P), None, ALU.mult))
                settle(ve.tensor_tensor(slot, te(bank[0][:, 0:NE]), incl[:, PAD - 1:PAD + NT - 1, :], ALU.add))
                settle(ve.tensor_tensor(slot, slot, start.unsqueeze(1).to_broadcast(S3), ALU.add))
                for k in range(TOPK):
                    settle(ve.tensor_tensor(te(A[2]), slot, te(oh[k]), ALU.mult))
                    settle(ve.tensor_reduce(slot_f[:, k * NT:(k + 1) * NT], te(A[2]), AX.X, ALU.add))
                settle(ve.tensor_copy(slot_i[:, :], slot_f[:, :]))
                settle(ve.tensor_scalar(r_i[:, :], slot_i[:, :], P - 1, None, ALU.bitwise_and))
                settle(ve.tensor_scalar(b_i[:, :], slot_i[:, :], 7, None, ALU.logical_shift_right))
                settle(ve.tensor_copy(r_h, r_i[:, :]))
                settle(ve.tensor_copy(b_h, b_i[:, :]))
                ecmp = work[:, 2048:2048 + NBP * E].rearrange("p (b e) -> p b e", e=E)
                she = [P, NBP, E]
                eb = work[:, 3072:3072 + NBP]
                settle(ve.tensor_tensor(ecmp, kc(C_B, NBP).unsqueeze(2).to_broadcast(she), end.unsqueeze(1).to_broadcast(she), ALU.is_ge))
                settle(ve.tensor_reduce(eb, ecmp, AX.X, ALU.add))
                settle(ve.tensor_scalar(eb, eb, float(E - 1), None, ALU.min))
                settle(ve.tensor_copy(eid[0:1, EIDS:EIDS + NBP], eb[0:1, :]))
                settle(ve.tensor_scalar(eoh[:, :], eb, keep[:, C_EMOD:C_EMOD + 1], None, ALU.is_equal))
                NK = TOPK * NT
                ohr = work[:, 0:2048].bitcast(BF16).rearrange("p (n r) -> p n r", r=P)
                obv = work[:, 2048:2048 + NBP * NK].bitcast(BF16).rearrange("p (n v b) -> p n v b", v=2, b=NBP)
                shb = [P, NK, NBP]
                settle(ve.tensor_tensor(ohr, cnt16[:, 0:P].unsqueeze(1).to_broadcast([P, NK, P]), r_h.unsqueeze(2).to_broadcast([P, NK, P]), ALU.is_equal))
                ob = work[:, 3584:3584 + NBP * NK // 2].bitcast(BF16).rearrange("p (n b) -> p n b", b=NBP)
                settle(ve.tensor_tensor(ob, cnt16[:, 0:NBP].unsqueeze(1).to_broadcast(shb), b_h.unsqueeze(2).to_broadcast(shb), ALU.is_equal))
                settle(ve.tensor_tensor(obv[:, :, 0, :], ob, cnt16[:, P:P + NK].unsqueeze(2).to_broadcast(shb), ALU.mult))
                ve.tensor_scalar(obv[:, :, 1, :], ob, keep[:, C_P:C_P + 1], None, ALU.mult).then_inc(onehot_s, 1)

            def route_index(l):
                tk, pos, row, none = (work[:, 64 * n:64 * n + NBP] for n in range(4))
                ri = work[:, 256:256 + NBP].bitcast(I32)
                ni = work[:, 320:320 + NBP].bitcast(I32)
                ve.wait_ge(table_s, l + 1)
                settle(ve.tensor_copy(tk, bank[0][:, 0:NBP]))
                settle(ve.tensor_scalar(none, tk, 0.0, float(OUTSIDE), ALU.is_equal, ALU.mult))
                settle(ve.tensor_scalar(row, tk, -1.0, float(P), ALU.add, ALU.mult))
                settle(ve.tensor_tensor(row, row, bank[0][:, NBP:2 * NBP], ALU.add))
                settle(ve.tensor_scalar(row, row, 0.0, None, ALU.max))
                settle(ve.tensor_tensor(pos, row, none, ALU.add))
                settle(ve.tensor_copy(sidx[:, :], pos))
                settle(ve.tensor_scalar(pos, row, float(T), -float(T), ALU.is_ge, ALU.mult))
                settle(ve.tensor_tensor(row, row, pos, ALU.add))
                settle(ve.tensor_tensor(row, row, none, ALU.add))
                ve.tensor_copy(gidx[:, :], row).then_inc(index_s, 1)

            def block_h(l, b, s):
                ve.wait_ge(esilu_s, b + (l * NB + 1))
                ve.tensor_tensor(e_h[:, s, :], e_silu[:, s, :], bank[3 + s][:, FI:2 * FI], ALU.mult).then_inc(eh_s, 1)

            def block_hT(l, b, s):
                ve.wait_ge(ehT_s, b + (l * NB + 1))
                settle_step(ve.tensor_copy(e_hT[:, s, 0, :], bank[5][:, 0:P]), l, b)
                ve.tensor_tensor(e_hT[:, s, 1, :], bank[5][:, 0:P], e_hT[:, s, 0, :], ALU.subtract).then_inc(ehTc_s, 1)

            def settle_step(ins, l, b):
                ins.then_inc(ehhi_s, 1)
                ve.wait_ge(ehhi_s, b + (l * NB + 1))

            def block_low(l, b, s):
                ve.wait_ge(gTc_s, b + (l * NB + 1))
                ve.tensor_tensor(xgT[:, s, :, 1, :], bank[s][:, :].rearrange("p (c n) -> p c n", c=KC), xgT[:, s, :, 0, :],
                                 ALU.subtract).then_inc(glo_s, 1)

            def block_out(l, b, r):
                ve.wait_ge(ed_s, b + (l * NB + 1))
                if not (l == 0 and isinstance(b, int) and b < RING):
                    ve.wait_ge(put_s[r], ring_count(l, b, r))
                ve.tensor_copy(yo[:, r, :], bank[6 + r % 2][:, :]).then_inc(yo_s, 1)

            def experts(l):
                def step(b, r):
                    block_h(l, b, r % 2)
                    if not (isinstance(b, int) and b == NB - 1):
                        block_low(l, b + 1, (r + 1) % 2)
                    if not (isinstance(b, int) and b == 0):
                        block_out(l, b - 1, (r - 1) % RING)
                    block_hT(l, b, r % 2)

                first = 2 * RING - 2
                last = (NB - 1 - first) // RING * RING + first
                block_low(l, 0, 0)
                for b in range(first):
                    step(b, b % RING)
                with ve.Fori(0, (last - first) // RING) as n:
                    b = n * RING + first
                    for u in range(RING):
                        step(b + u, (first + u) % RING)
                for b in range(last, NB):
                    step(b, b % RING)
                block_out(l, NB - 1, (NB - 1) % RING)

            stats("f0", 0)
            for i in range(GT):
                normalize("f0", 0, i)
            once = lambda c, n: work[:, c:c + n]

            def bias_parts(dst, col, n, mask, scratch):
                raw = once(col, n)
                hi, mid = (work[:, c:c + n // 2].bitcast(BF16) for c in scratch)
                acc = work[:, 1280:1280 + n]
                m = [keep[:, mask + k:mask + k + 1] for k in range(3)]
                settle(ve.tensor_copy(hi, raw))
                settle(ve.tensor_tensor(raw, raw, hi, ALU.subtract))
                settle(ve.tensor_copy(mid, raw))
                settle(ve.tensor_tensor(raw, raw, mid, ALU.subtract))
                settle(ve.tensor_scalar(acc, hi, m[0], None, ALU.mult))
                settle(ve.scalar_tensor_tensor(out=acc, in0=mid, scalar=m[1], in1=acc, op0=ALU.mult, op1=ALU.add))
                settle(ve.scalar_tensor_tensor(out=acc, in0=raw, scalar=m[2], in1=acc, op0=ALU.mult, op1=ALU.add))
                return ve.tensor_copy(dst, acc)

            low_part("f0", 0, 0)
            low_part("f0", 0, 1)
            low_parts(0, 1)
            low_part("f0", 0, 2)
            low_part("f0", 0, 3)
            ve.tensor_scalar(kc(C_SB2, SF), kc(C_SB2, SF), WS, None, ALU.mult).then_inc(sb2_s, 1)
            low_parts(1, KC)
            stats("f0", 1)
            for i in range(GT):
                normalize("f0", 1, i)
            stats("f0", 2)
            low_part("f0", 1, 0)
            low_part("f0", 1, 1)
            for i in range(GT):
                normalize("f0", 2, i)
            low_part("f0", 1, 2)
            low_part("f0", 1, 3)
            stats("f0", 3)
            low_parts(1 + KC, SF)
            low_part("f0", 2, 0)
            low_part("f0", 2, 1)
            low_parts(SMALL, PIECES[0][2])
            low_part("f0", 2, 2)
            low_part("f0", 2, 3)
            for i in range(GT):
                normalize("f0", 3, i)
            ve.wait_ge(once_s, 16)
            ve.wait_ge(consts_s, 1)
            ve.tensor_copy(cnt16[:, 0:P], once(S_R, P))
            ve.tensor_copy(cnt16[:, P:], kc(C_TK, TOPK * NT))
            ve.tensor_copy(tri[:, :], once(S_TRI, P))
            ve.tensor_copy(sel_bv[:, :], once(S_SELV, P))
            ve.memset(ones[:, :], 1.0)
            settle(bias_parts(b12[:, :], S_B12, 2 * FI, C_MASK, (1792, 1920)))
            for i in range(GT):
                low_part("f0", 3, i)
                low_parts(SMALL + sum(PIECES[0][:2 * SF + i]), PIECES[0][2 * SF + i])
            for s in range(2, len(xn_slots)):
                ve.wait_ge(xn_out[s], 16 * stores_from(s, range(NT)))
            route_choose(0, range(SMALL + CUTS[1], SMALL + CUTS[2]))
            assert not beside
            beside += range(SMALL + CUTS[2], SMALL + CUTS[3])
            route_slots(0)
            assert not beside
            route_index(0)
            low_parts(SMALL + CUTS[3], NP - CUTS[3])
            experts(0)
            for i in range(GT):
                combine(0, i)
                tile_stats("a", 0, i)
            group_stats("a", 0)
            for i in range(GT):
                normalize("a", 0, i)
            for i in range(GT):
                combine(0, GT + i)
                tile_stats("a", 1, i)
            group_stats("a", 1)
            for g in range(G):
                attention(g)
            for i in range(GT):
                normalize("f1", G - 1, i)
                if i:
                    low_part("f1", G - 1, i - 1)
            low_part("f1", G - 1, GT - 1)
            route_choose(1)
            route_slots(1)
            route_index(1)
            experts(1)
            for t in range(NT):
                combine(1, t)


def kernel(**inputs):
    import numpy as np
    import concourse.bacc as bacc
    from concourse.bass_utils import run_bass_kernel_spmd

    a = {k.removeprefix("L0_"): np.asarray(v, dtype=None) for k, v in inputs.items()}
    f32 = np.float32
    keep = np.zeros((P, NKEEP), f32)
    p = np.arange(P)
    keep[:, C_ID:C_ID + P] = np.eye(P, dtype=f32)
    keep[:, C_B:C_B + NBP] = np.arange(NBP)
    keep[:, C_REV16:C_REV16 + 16] = 16 - np.arange(16)
    keep[:, C_REV4:C_REV4 + 4] = 4 - np.arange(4)
    keep[:, C_THR:C_THR + 16] = P * np.arange(16)
    keep[:, C_TK:C_TK + 32] = 1 + np.arange(32)
    keep[:, C_P] = p
    keep[:, C_EMOD] = np.where(p < 3 * E, p % E, -1)
    part = np.full(P, -1)
    part[:3 * E] = np.arange(3 * E) // E
    part[3 * E:3 * E + 6] = np.arange(6) % 3
    for n in range(3):
        keep[:, C_MASK + n] = (part == n) * np.where(p < 3 * E, WS, 1)
        keep[:, C_MASK3 + n] = (part == n) * WS * WS
    keep[:, C_SB1:C_SB1 + 2] = a["ffn_sb1"].reshape(SF, P).T
    keep[:, C_SB2:C_SB2 + 2] = a["ffn_sb2"].reshape(SF, P).T
    keep[:, C_BQKV:C_BQKV + 3] = a["attn_bqkv"].reshape(3, HD).T
    keep[:, C_RB:C_RB + E] = a["ffn_router_b"]
    keep[:, C_RBIAS:C_RBIAS + E] = a["ffn_router_bias"]
    once = np.zeros((P, NONCE), f32)
    once[:, S_R:S_R + P] = np.arange(P)
    once[:, S_TRI:S_TRI + P] = p[:, None] < p[None, :]
    once[3 * E:3 * E + 3, S_SELS:S_SELS + P] = 1
    once[3 * E + 3:3 * E + 6, S_SELV:S_SELV + P] = 1
    for n in range(3):
        once[n * E:(n + 1) * E, S_B12:S_B12 + FI] = a["ffn_eb1"]
        once[n * E:(n + 1) * E, S_B12 + FI:S_B12 + 2 * FI] = a["ffn_eb2"]
        once[n * E:(n + 1) * E, S_B3:S_B3 + D] = a["ffn_eb3"]
    once[3 * E:3 * E + 3, S_B3:S_B3 + D] = a["ffn_sb3"]
    once[3 * E + 3:3 * E + 6, S_B12:S_B12 + HD] = a["attn_bqkv"][2 * HD:]

    chunks = lambda w: w.reshape(-1, P, w.shape[-1]).transpose(1, 0, 2)
    both = np.stack([a["ffn_ew1"], a["ffn_ew2"]], axis=2)
    arrays = {
        "x_in": a["attn_x"].reshape(T, D),
        "keep_in": keep,
        "once_in": once,
        "rw_in": chunks(a["ffn_router_w"]),
        "w12_in": both.reshape(E, KC, P, 2 * FI).transpose(2, 1, 0, 3).reshape(P, KC * E * 2 * FI),
        "w3_in": a["ffn_ew3"].transpose(1, 0, 2).reshape(P, E * D),
        "sw12_in": chunks(np.concatenate([a["ffn_sw1"], a["ffn_sw2"]], axis=1)),
        "sw3_in": chunks(a["ffn_sw3"]),
        "wqkv_in": chunks(a["attn_Wqkv"]),
        "wo_in": a["attn_Wo"],
        "bo_in": np.broadcast_to(a["attn_bo"], (P, D)),
    }
    arrays = {k: np.ascontiguousarray(v) for k, v in arrays.items()}
    nc = bacc.Bacc("TRN2", target_bir_lowering=False, num_devices=1)
    ins = [nc.dram_tensor(k, v.shape, mybir.dt.from_np(v.dtype), kind="ExternalInput").ap() for k, v in arrays.items()]
    out = nc.dram_tensor("out", (T, D), mybir.dt.float32, kind="ExternalOutput").ap()
    macaron_kernel(nc, *ins, out)
    r = run_bass_kernel_spmd(nc, [arrays], core_ids=[0])
    return r.results[0]["out"].reshape(G, GW, D)
```
